# Optimizing a Trainium2 kernel written in Bass

```python
import numpy as np
import jax
import jax.numpy as jnp

def _softmax(x, axis=-1):
    return jax.nn.softmax(x, axis=axis)

def _gelu(x):
    return jax.nn.gelu(x, approximate=True)

def _silu(x):
    return jax.nn.silu(x)

def _sigmoid(x):
    return jax.nn.sigmoid(x)

def _layernorm(x, axis=-1, eps=1e-05):
    m = jnp.mean(x, axis=axis, keepdims=True)
    v = jnp.var(x, axis=axis, keepdims=True)
    return (x - m) / jnp.sqrt(v + eps)

def _scatter_add(tgt, idx, src, axis=0):
    return tgt.at[idx].add(src)

def _segment_sum(src, seg, n):
    return jax.ops.segment_sum(src, seg, n)
kernel_name = 'mk_decoder_preln_d1_seqx_r4_d85932'

def setup_inputs(seed: int=0):
    np.random.seed(seed)
    _w = jnp.asarray

    def _rec_inputs():
        import jax
        import jax.numpy as jnp
        _rk = jax.random.key(seed)
        x = 0.0002417 + 0.9998 * jax.random.normal(jax.random.fold_in(_rk, 1), (4, 512, 256), jnp.float32)
        _lenS = 512 - jax.random.randint(jax.random.fold_in(_rk, 7), (4,), 0, max(1, 512 // 4) + 1, jnp.int32)
        _lenS2 = 64 - jax.random.randint(jax.random.fold_in(_rk, 8), (4,), 0, max(1, 64 // 4) + 1, jnp.int32)
        _ctx_1024P = jax.random.normal(jax.random.fold_in(_rk, 11), (4, 16, 256), jnp.float32)
        _ctx_1024c = jax.random.dirichlet(jax.random.fold_in(_rk, 511), 0.3 * jnp.ones((16,), jnp.float32), (4, 64))
        _ctx_1024t = jnp.einsum('bsk,bkd->bsd', _ctx_1024c, _ctx_1024P)
        _ctx_1024t = _ctx_1024t * jax.lax.rsqrt(jnp.mean(jnp.square(_ctx_1024t)) + 1e-12) * 0.953939
        ctx_1024 = 7.22013e-05 + 1.00017 * (_ctx_1024t + 0.3 * jax.random.normal(jax.random.fold_in(_rk, 611), (4, 64, 256), jnp.float32))
        return (x, ctx_1024)
    x, ctx_1024 = _rec_inputs()

    def _L0_attn_setup():
        import jax, jax.numpy as jnp
        import numpy as np
        KEY_DIM = 16
        key = jax.random.key(seed)
        k1, k2, k3, k4, k5 = jax.random.split(key, 5)
        B, N, D, H, KD, VD = (2, 512, 256, 16, 16, 64)
        return {'x': jax.random.normal(k1, (B, N, D), dtype=jnp.float32), 'query_proj': jax.random.normal(k2, (H, KD, D), dtype=jnp.float32) * 0.02, 'key_proj': jax.random.normal(k3, (H, KD, D), dtype=jnp.float32) * 0.02, 'value_proj': jax.random.normal(k4, (H, VD, D), dtype=jnp.float32) * 0.02, 'output_proj': jax.random.normal(k5, (D, H, VD), dtype=jnp.float32) * 0.02}
    _L0_attn_all = _L0_attn_setup()
    _L0_attn_in = {k: v for k, v in _L0_attn_all.items() if k in ('query_proj', 'key_proj', 'value_proj', 'output_proj')}
    del _L0_attn_all

    def _L0_xattn_setup():
        import jax, jax.numpy as jnp
        import numpy as np
        EMBED = 256
        HEADS = 16
        HEAD_DIM = EMBED // HEADS
        EXP_DIM = 2 * HEAD_DIM

        def _feature_map(x, fm_w, fm_b):
            z = jnp.einsum('nshd,ed->nshe', x, fm_w) + fm_b
            return jnp.concatenate([jnp.exp(z), jnp.exp(-z)], axis=-1)
        key = jax.random.key(seed)
        ks = jax.random.split(key, 7)
        N, S = (4, 512)
        values = jax.random.normal(ks[0], (N, S, EMBED), dtype=jnp.float32)
        keys_ = jax.random.normal(ks[1], (N, S, EMBED), dtype=jnp.float32)
        query = jax.random.normal(ks[2], (N, S, EMBED), dtype=jnp.float32)
        fm_w = jnp.eye(HEAD_DIM, dtype=jnp.float32) + 0.02 * jax.random.normal(ks[3], (HEAD_DIM, HEAD_DIM), dtype=jnp.float32)
        fm_b = 0.02 * jax.random.normal(ks[4], (HEAD_DIM,), dtype=jnp.float32)
        fc_w = jax.random.normal(ks[5], (EMBED, HEADS * EXP_DIM), dtype=jnp.float32) * (1.0 / np.sqrt(HEADS * EXP_DIM))
        fc_b = jnp.zeros((EMBED,), dtype=jnp.float32)
        return {'values': values, 'keys': keys_, 'query': query, 'fm_w': fm_w, 'fm_b': fm_b, 'fc_w': fc_w, 'fc_b': fc_b}
    _L0_xattn_all = _L0_xattn_setup()
    _L0_xattn_in = {k: v for k, v in _L0_xattn_all.items() if k in ('fm_w', 'fm_b', 'fc_w', 'fc_b')}
    del _L0_xattn_all

    def _L0_ffn_setup():
        import jax, jax.numpy as jnp
        import numpy as np
        DIM = 256

        def _reference_tuple_inner(x, W_r, W_k, W_v, mu_r, mu_k):
            B, T, C = x.shape
            x_prev = jnp.concatenate([jnp.zeros((B, 1, C), x.dtype), x[:, :-1, :]], axis=1)
            xr = mu_r * x + (1.0 - mu_r) * x_prev
            xk = mu_k * x + (1.0 - mu_k) * x_prev
            r = jax.nn.sigmoid(jnp.einsum('btc,dc->btd', xr, W_r))
            k = jnp.einsum('btc,dc->btd', xk, W_k)
            k_act = jnp.square(jax.nn.relu(k))
            out = r * jnp.einsum('btc,dc->btd', k_act, W_v)
            new_state = x[:, -1, :]
            return (out, new_state)
        key = jax.random.key(seed)
        ks = jax.random.split(key, 6)
        B, T, C = (8, 512, DIM)
        x = jax.random.normal(ks[0], (B, T, C), dtype=jnp.float32)
        s = 1.0 / np.sqrt(C)
        W_r = jax.random.uniform(ks[1], (C, C), jnp.float32, -s, s)
        W_k = jax.random.uniform(ks[2], (C, C), jnp.float32, -s, s)
        W_v = jax.random.uniform(ks[3], (C, C), jnp.float32, -s, s)
        mu_r = jax.random.uniform(ks[4], (C,), jnp.float32)
        mu_k = jax.random.uniform(ks[5], (C,), jnp.float32)
        return {'x': x, 'W_r': W_r, 'W_k': W_k, 'W_v': W_v, 'mu_r': mu_r, 'mu_k': mu_k}
    _L0_ffn_all = _L0_ffn_setup()
    _L0_ffn_in = {k: v for k, v in _L0_ffn_all.items() if k in ('W_r', 'W_k', 'W_v', 'mu_r', 'mu_k')}
    del _L0_ffn_all
    return {'x': x, 'ctx_1024': ctx_1024, 'L0_attn_query_proj': _L0_attn_in['query_proj'], 'L0_attn_key_proj': _L0_attn_in['key_proj'], 'L0_attn_value_proj': _L0_attn_in['value_proj'], 'L0_attn_output_proj': _L0_attn_in['output_proj'], 'L0_xattn_fm_w': _L0_xattn_in['fm_w'], 'L0_xattn_fm_b': _L0_xattn_in['fm_b'], 'L0_xattn_fc_w': _L0_xattn_in['fc_w'], 'L0_xattn_fc_b': _L0_xattn_in['fc_b'], 'L0_ffn_W_r': _L0_ffn_in['W_r'], 'L0_ffn_W_k': _L0_ffn_in['W_k'], 'L0_ffn_W_v': _L0_ffn_in['W_v'], 'L0_ffn_mu_r': _L0_ffn_in['mu_r'], 'L0_ffn_mu_k': _L0_ffn_in['mu_k']}

def reference(x, ctx_1024, L0_attn_query_proj, L0_attn_key_proj, L0_attn_value_proj, L0_attn_output_proj, L0_xattn_fm_w, L0_xattn_fm_b, L0_xattn_fc_w, L0_xattn_fc_b, L0_ffn_W_r, L0_ffn_W_k, L0_ffn_W_v, L0_ffn_mu_r, L0_ffn_mu_k):
    import jax
    import jax.numpy as jnp

    def _L0_attn_ref(x, query_proj, key_proj, value_proj, output_proj):
        import jax, jax.numpy as jnp
        import numpy as np
        KEY_DIM = 16
        q = jnp.einsum('bnd,hkd->bnhk', x, query_proj)
        k = jnp.einsum('bnd,hkd->bnhk', x, key_proj)
        v = jnp.einsum('bnd,hvd->bnhv', x, value_proj)
        sim = jnp.einsum('bnkh,bmhk->bnhm', q, k)
        scale = jnp.asarray(1.0 / np.sqrt(KEY_DIM), dtype=sim.dtype)
        attn = jax.nn.softmax(sim * scale, axis=1)
        o = jnp.einsum('bnhm,bmhv->bnhv', attn, v)
        return jnp.einsum('bnhv,dhv->bnd', o, output_proj)

    def _L0_xattn_ref(values, keys, query, fm_w, fm_b, fc_w, fc_b):
        import jax, jax.numpy as jnp
        import numpy as np
        EMBED = 256
        HEADS = 16
        HEAD_DIM = EMBED // HEADS
        EXP_DIM = 2 * HEAD_DIM

        def _feature_map(x, fm_w, fm_b):
            z = jnp.einsum('nshd,ed->nshe', x, fm_w) + fm_b
            return jnp.concatenate([jnp.exp(z), jnp.exp(-z)], axis=-1)
        N, S, _ = query.shape
        v = values.reshape(N, -1, HEADS, HEAD_DIM)
        k = keys.reshape(N, -1, HEADS, HEAD_DIM)
        q = query.reshape(N, -1, HEADS, HEAD_DIM)
        v, k, q = (_feature_map(x, fm_w, fm_b) for x in (v, k, q))
        scores = jnp.einsum('nqhd,nkhd->nhqk', q, k) / jnp.sqrt(jnp.float32(EMBED))
        attn = jax.nn.softmax(scores, axis=-1)
        out = jnp.einsum('nhql,nlhd->nqhd', attn, v)
        out = out.reshape(N, S, HEADS * EXP_DIM)
        return out @ fc_w.T + fc_b

    def _L0_ffn_ref(x, W_r, W_k, W_v, mu_r, mu_k):
        import jax, jax.numpy as jnp
        import numpy as np
        DIM = 256

        def _reference_tuple_inner(x, W_r, W_k, W_v, mu_r, mu_k):
            B, T, C = x.shape
            x_prev = jnp.concatenate([jnp.zeros((B, 1, C), x.dtype), x[:, :-1, :]], axis=1)
            xr = mu_r * x + (1.0 - mu_r) * x_prev
            xk = mu_k * x + (1.0 - mu_k) * x_prev
            r = jax.nn.sigmoid(jnp.einsum('btc,dc->btd', xr, W_r))
            k = jnp.einsum('btc,dc->btd', xk, W_k)
            k_act = jnp.square(jax.nn.relu(k))
            out = r * jnp.einsum('btc,dc->btd', k_act, W_v)
            new_state = x[:, -1, :]
            return (out, new_state)
        return _reference_tuple_inner(x, W_r, W_k, W_v, mu_r, mu_k)[0]
    x = x + _L0_attn_ref(_layernorm(x, axis=-1), L0_attn_query_proj, L0_attn_key_proj, L0_attn_value_proj, L0_attn_output_proj)
    x = x + _L0_xattn_ref(ctx_1024, ctx_1024, _layernorm(x, axis=-1), L0_xattn_fm_w, L0_xattn_fm_b, L0_xattn_fc_w, L0_xattn_fc_b)
    x = x + _L0_ffn_ref(_layernorm(x, axis=-1), L0_ffn_W_r, L0_ffn_W_k, L0_ffn_W_v, L0_ffn_mu_r, L0_ffn_mu_k)
    return x

_drawn_inputs = setup_inputs


def setup_inputs(seed=0):
    import zlib

    import numpy as np

    out = dict(_drawn_inputs(seed))
    spreads = {'L0_xattn_fc_b': (0.0, 0.747)}
    factors = {'L0_attn_query_proj': 8.0,
     'L0_attn_key_proj': 8.0,
     'L0_attn_value_proj': 7.287,
     'L0_attn_output_proj': 7.612,
     'L0_ffn_W_r': 8.0,
     'L0_ffn_W_k': 5.746,
     'L0_ffn_W_v': 5.421,
     'L0_ffn_mu_r': 8.0,
     'L0_ffn_mu_k': 8.0}
    for name, (base, spread) in spreads.items():
        noise = np.random.default_rng([zlib.crc32(name.encode()), seed]).standard_normal(out[name].shape)
        drawn = base * np.exp(spread * noise) if base else spread * noise
        out[name] = jnp.asarray(drawn.astype(out[name].dtype))
    for name, factor in factors.items():
        out[name] = (out[name] * factor).astype(out[name].dtype)
    return out
```

```python
from contextlib import ExitStack

import concourse.bass as bass
from concourse import mybir

F32 = mybir.dt.float32
F32R = mybir.dt.float32r
ALU = mybir.AluOpType
ACT = mybir.ActivationFunctionType
AX_X = mybir.AxisListType.X

P = 128
B, N, D = 4, 512, 256
H, KD, VD = 16, 16, 64
L, FE = 64, 32
EPS = 1e-5
DC = D // P
NT = N // P
NP = H // 2
HALF = N // 2
STEPS = NP * NT * 2
TILES = B * STEPS
S_BANKS, AV_BANKS, MISC_BANKS = 3, 2, 3
E_RING = 8
STACK = 4
AV_LAG, SCALE_LAG = 6, 2
OE_LAG = 2 * NT + AV_LAG - 1

BANKED = {"t1", "qk", "v", "op", "t2", "kv", "kf", "z", "xs", "pt", "pv", "fc", "t3", "fr", "fk", "fv"}

PLAN = [
    (1, "qk", 0, (1, 0)), (2, "qk_lo", 0, (1, 0)),
    (3, "qk", 0, (1, 1)), (4, "qk_lo", 0, (1, 1)),
    (1, "ld", 0, (3,)), (9, "ld", 0, (4,)), (17, "ld", 0, (5,)), (25, "ld", 0, (6,)), (33, "ld", 0, (7,)),
    (8, "op", -1, (1, 0)), (9, "ln2", -1, (0,)), (10, "op", -1, (1, 1)), (12, "ln2", -1, (1,)),
    (6, "kv", -1, ()),
    (7, "v", 0, (1, 0)), (9, "v", 0, (1, 1)), (12, "t2", -1, (0,)), (16, "t2", -1, (1,)),
    (13, "v", 0, (1, 2)), (14, "z", -1, (0, 0)), (15, "z", -1, (0, 1)),
    (17, "v", 0, (1, 3)), (22, "z", -1, (1, 0)), (23, "z", -1, (1, 1)),
    (18, "xs", -1, (0, 0)), (19, "xs", -1, (0, 1)), (20, "xs", -1, (1, 0)), (21, "xs", -1, (1, 1)),
    (20, "xn", -1, (0, 0)), (21, "xn", -1, (0, 1)), (22, "xn", -1, (1, 0)), (23, "xn", -1, (1, 1)),
    (23, "pt", -1, (0, 0)), (24, "pt", -1, (0, 1)), (25, "xs", -1, (2, 0)), (25, "pt", -1, (1, 0)),
    (26, "xs", -1, (2, 1)), (26, "pt", -1, (1, 1)), (27, "xn", -1, (2, 0)), (28, "xn", -1, (2, 1)),
    (27, "pv", -1, (0, 0)), (28, "pv", -1, (0, 1)),
    (28, "xs", -1, (3, 0)), (29, "xs", -1, (3, 1)), (30, "xn", -1, (3, 0)), (31, "xn", -1, (3, 1)),
    (30, "pt", -1, (2, 0)), (31, "pt", -1, (2, 1)), (31, "fc", -1, (0,)), (32, "ln3", -1, (0,)),
    (33, "pt", -1, (3, 0)), (34, "pt", -1, (3, 1)), (35, "t3", -1, (0,)), (36, "mix", -1, (0,)),
    (35, "pv", -1, (1, 0)), (36, "pv", -1, (1, 1)), (38, "fc", -1, (1,)), (39, "ln3", -1, (1,)),
    (33, "ln1", 1, (0,)), (38, "ln1", 1, (1,)),
    (37, "t1", 1, (0,)), (38, "t1_lo", 1, (0,)), (39, "t1", 1, (1,)), (40, "t1_lo", 1, (1,)),
    (40, "op", 0, (0, 0)), (42, "op", 0, (0, 1)),
    (41, "fr", -1, (0,)), (42, "fk", -1, (0,)),
    (43, "t3", -1, (1,)), (44, "mix", -1, (1,)),
    (44, "qk", 1, (0, 0)), (45, "qk_lo", 1, (0, 0)), (46, "qk", 1, (0, 1)), (47, "qk_lo", 1, (0, 1)),
    (48, "fv", -1, (0,)), (50, "fr", -1, (1,)), (51, "fk", -1, (1,)), (57, "fv", -1, (1,)),
    (52, "ld", 1, (0,)), (53, "ld", 1, (1,)), (57, "ld", 1, (2,)),
    (52, "v", 1, (0, 0)), (54, "v", 1, (0, 1)), (59, "v", 1, (0, 2)), (61, "v", 1, (0, 3)),
]
FIRST = [
    ("ln1", 0, (0,)), ("ln1", 0, (1,)), ("cut", 0, ("qk",)),
    ("t1", 0, (0,)), ("t1_lo", 0, (0,)), ("t1", 0, (1,)), ("t1_lo", 0, (1,)),
    ("qk", 0, (0, 0)), ("qk_lo", 0, (0, 0)), ("qk", 0, (0, 1)), ("qk_lo", 0, (0, 1)),
    ("ld", 0, (0,)), ("ld", 0, (1,)), ("ld", 0, (2,)),
    ("cut", 0, ("v",)),
    ("v", 0, (0, 0)), ("v", 0, (0, 1)), ("v", 0, (0, 2)), ("v", 0, (0, 3)),
    ("feat", 0, ()), ("kf", 0, (0,)), ("kf", 0, (1,)), ("cut", 0, ("o",)),
]


def schedule():
    rounds = [(-1, FIRST)]
    for r in range(B + 1):
        for step in range(STEPS):
            stages = [(name, r + off, args) for at, name, off, args in sorted(PLAN, key=lambda e: e[0])
                      if at == step and 0 <= r + off < B]
            rounds.append((r * STEPS + step, stages))
    return rounds


def bank_uses(steps):
    uses, n = {}, 0
    for _, stages in steps:
        for unit in stages:
            if unit[0] in BANKED:
                uses[unit] = (n % MISC_BANKS, n // MISC_BANKS)
                n += 1
    return uses


def build(nc, x, ctx_t, wqk, wv, wo, fm_t, fm_b, wfc, fc_b, wffn, mu, ident, sign, out):
    steps = schedule()
    uses = bank_uses(steps)

    with ExitStack() as ctx:
        def sb(name, shape, dt=F32):
            return ctx.enter_context(nc.sbuf_tensor(name, shape, dt))

        def sem(name):
            return ctx.enter_context(nc.semaphore(name))

        x_sb = sb("x_sb", [P, B * NT, D])
        wqk_hi, wqk_lo = sb("wqk_hi", [P, DC, 2 * H * KD], F32R), sb("wqk_lo", [P, DC, 2 * H * KD], F32R)
        wv_hi, wv_lo = sb("wv_hi", [P, DC, H * VD], F32R), sb("wv_lo", [P, DC, H * VD], F32R)
        wo_hi, wo_lo = sb("wo_hi", [P, NP, D], F32R), sb("wo_lo", [P, NP, D], F32R)
        wfc_sb = sb("wfc_sb", [P, 4, D])
        wffn_sb = sb("wffn_sb", [P, 3, DC, D])
        fm_sb = sb("fm_sb", [P, 2, 4, 2, KD])
        fmb = sb("fmb", [P, 1])
        fcb = sb("fcb", [P, D])
        mu_sb = sb("mu_sb", [P, 2, DC])
        id_sb = sb("id_sb", [P, P])
        sign_sb = sb("sign_sb", [P, 1])
        power = sb("power", [P, 2])
        xn = [sb("xn1", [P, 2, D]), sb("xn23", [P, 2, D])]
        stats = [sb("stats1", [P, 2, 6]), sb("stats23", [P, 2, 6])]
        mv = [sb("mv1", [P, 2, 2]), sb("mv23", [P, 2, 2])]
        nmean = [sb("nmean1", [P, 2]), sb("nmean23", [P, 2])]
        veps = [sb("veps1", [P, 2]), sb("veps23", [P, 2])]
        rstd = [sb("rstd1", [P, 2]), sb("rstd23", [P, 2])]
        xt_hi, xt_lo = sb("xt_hi", [P, DC, N], F32R), sb("xt_lo", [P, DC, N], F32R)
        qkt_hi, qkt_lo = sb("qkt_hi", [P, 2, N], F32R), sb("qkt_lo", [P, 2, N], F32R)
        q_st, k_st = sb("q_st", [P, STACK, N], F32R), sb("k_st", [P, STACK, N], F32R)
        v_sb = sb("v_sb", [P, NT, H, VD])
        e_sb = sb("e_sb", [P, E_RING, N])
        nmax = sb("nmax", [P, E_RING])
        esum = sb("esum", [P, 2 * E_RING])
        rsum = sb("rsum", [P, 4, 2])
        ot_hi, ot_lo = sb("ot_hi", [P, 4, N], F32R), sb("ot_lo", [P, 4, N], F32R)
        kf = sb("kf", [P, 4, B, 2, L])
        kblk = sb("kblk", [P, 4, 4, L])
        vblk = sb("vblk", [P, NP, 2 * FE])
        xt2 = sb("xt2", [P, DC, HALF])
        qf = sb("qf", [P, 4, HALF])
        sx = sb("sx", [P, 4, 512])
        xmax = sb("xmax", [P, 4, 8])
        xsum = sb("xsum", [P, 4, 8])
        xrec = sb("xrec", [P, 4, 8])
        pt_sb = sb("pt_sb", [P, NP, HALF])
        oxt = sb("oxt", [P, 4, HALF])
        xt3 = sb("xt3", [P, DC, 1 + N])
        mix_r, mix_k = sb("mix_r", [P, DC, HALF]), sb("mix_k", [P, DC, HALF])
        gate = sb("gate", [P, 2, D])
        kact = sb("kact", [P, DC, HALF])
        wqk_raw = qf[:, :, :].rearrange("p g n -> p (g n)").rearrange("p (c n) -> p c n", c=DC)
        wv_raw = sx[:, :, :].rearrange("p g n -> p (g n)").rearrange("p (c n) -> p c n", c=DC)
        wo_raw = pt_sb
        ctx_sb = oxt[:, 0:2, :]

        s_bank = [ctx.enter_context(nc.psum_tensor(f"s_bank{i}", [P, 512], F32)) for i in range(S_BANKS)]
        av_bank = [ctx.enter_context(nc.psum_tensor(f"av_bank{i}", [P, 512], F32)) for i in range(AV_BANKS)]
        m_bank = [ctx.enter_context(nc.psum_tensor(f"m_bank{i}", [P, 512], F32)) for i in range(MISC_BANKS)]

        stacked = nc.dram_tensor("stacked", (2, 2, 8, 4, KD, N), F32, kind="Internal").ap()

        x_in = [sem(f"x_in{b}") for b in range(B)]
        wqk_in, wv_in, wo_in, id_in = sem("wqk_in"), sem("wv_in"), sem("wo_in"), sem("id_in")
        fm_zero, fm_in, ctx_in, post_in = sem("fm_zero"), sem("fm_in"), sem("ctx_in"), sem("post_in")
        stack_in = [[sem(f"{o}_stack_in{i}") for i in range(STACK)] for o in "qk"]
        stack_out = [[sem(f"{o}_parts_out{c}") for c in range(2)] for o in "qk"]
        res_out = sem("res_out")
        filled = [sem(f"filled{i}") for i in range(MISC_BANKS)]
        emptied = [sem(f"emptied{i}") for i in range(MISC_BANKS)]
        consts_set, wgt_hi, wgt_lo, fm_ready = sem("consts_set"), sem("wgt_hi"), sem("wgt_lo"), sem("fm_ready")
        var_ready = [sem("var_ready1"), sem("var_ready23")]
        rstd_ready = [sem("rstd_ready1"), sem("rstd_ready23")]
        xn_ready = [sem("xn_ready1"), sem("xn_ready23")]
        dve_chain, pool_chain = sem("dve_chain"), sem("pool_chain")
        xt_hi_ready, qk_hi_ready = sem("xt_hi_ready"), sem("qk_hi_ready")
        scores_ready, nmax_ready, exp_ready = sem("scores_ready"), sem("nmax_ready"), sem("exp_ready")
        rsum_ready, v_scaled, av_done = sem("rsum_ready"), sem("v_scaled"), sem("av_done")
        ot_hi_ready, ot_ready = sem("ot_hi_ready"), sem("ot_ready")
        bias_added, kblk_ready = sem("bias_added"), sem("kblk_ready")
        xexp_ready, xrec_ready, xp_ready = sem("xexp_ready"), sem("xrec_ready"), sem("xp_ready")
        mix_ready, relu_ready, kact_ready, res_ready = (sem("mix_ready"), sem("relu_ready"),
                                                        sem("kact_ready"), sem("res_ready"))

        block = ctx.enter_context(nc.Block())

        def bank(unit):
            return m_bank[uses[unit][0]]

        def wait_filled(eng, unit):
            i, before = uses[unit]
            eng.wait_ge(filled[i], before + 1)

        def wait_emptied(eng, unit):
            i, before = uses[unit]
            eng.wait_ge(emptied[i], before + 1)

        def wait_bank(eng, unit):
            i, before = uses[unit]
            if before:
                eng.wait_ge(emptied[i], before)

        def lagged(g):
            scale = (g - SCALE_LAG) // 2 if g >= SCALE_LAG and (g - SCALE_LAG) % 2 == 0 else None
            weigh = (g - AV_LAG) // 2 if g >= AV_LAG and (g - AV_LAG) % 2 == 0 else None
            high = (g - OE_LAG) // 8 if g >= OE_LAG and (g - OE_LAG) % 8 == 0 else None
            keep = lambda n, top: n if n is not None and n < top else None
            return keep(scale, TILES // 2), keep(weigh, TILES // 2), keep(high, B * NP)

        @block.sync
        def _(sp):
            xv = x.rearrange("(t p) d -> p t d", p=P)
            sp.dma_start(x_sb[:, 0:NT, :], xv[:, 0:NT, :]).then_inc(x_in[0], 16)
            sp.dma_start(wqk_raw, wqk).then_inc(wqk_in, 16)
            sp.dma_start(id_sb[:], ident).then_inc(id_in, 16)
            sp.dma_start(wv_raw, wv).then_inc(wv_in, 16)
            sp.dma_start(wo_raw[:], wo).then_inc(wo_in, 16)
            sp.dma_start(ctx_sb, ctx_t).then_inc(ctx_in, 16)
            sp.dma_start(sign_sb[:], sign).then_inc(fm_in, 16)
            sp.wait_ge(fm_zero, 1)
            for h in range(8):
                for s in range(2):
                    sp.dma_start(fm_sb[h * KD:(h + 1) * KD, h // 4, h % 4, s, :], fm_t).then_inc(fm_in, 16)
                sp.dma_start(fmb[h * KD:(h + 1) * KD, :], fm_b).then_inc(fm_in, 16)
            sp.dma_start(fcb[:], fc_b.partition_broadcast(P)).then_inc(post_in, 16)
            sp.dma_start(mu_sb[:], mu).then_inc(post_in, 16)
            sp.dma_start(wfc_sb[:], wfc).then_inc(post_in, 16)
            sp.dma_start(wffn_sb[:], wffn).then_inc(post_in, 16)
            for b in range(1, B):
                sp.dma_start(x_sb[:, b * NT:(b + 1) * NT, :], xv[:, b * NT:(b + 1) * NT, :]).then_inc(x_in[b], 16)

            def qk_lo(b, c, o):
                wait_emptied(sp, ("qk", b, (c, o)))
                if b:
                    for i in range(STACK):
                        sp.wait_ge(stack_in[o][i], 16 * ((b - 1) * 2 + c + 1))
                for blk in range(4):
                    part = (qkt_hi, qkt_lo)[blk % 2 if o == 0 else blk // 2]
                    sp.dma_start(stacked[o, c, :, blk], part[:, o, :].bitcast(F32)).then_inc(stack_out[o][c], 16)

            def ld(b, p):
                n = b * NP + p
                for o, st in ((0, q_st), (1, k_st)):
                    sp.wait_ge(stack_out[o][p // 4], 64 * (b + 1))
                    if n >= STACK and o == 0:
                        sp.wait_ge(scores_ready, 8 * (n - STACK + 1))
                    rows = stacked[o, p // 4].rearrange("h k i n -> (h k i) n")
                    at = (p % 4) * P
                    sp.dma_start(st[:, n % STACK, :].bitcast(F32), rows[at:at + P, :]).then_inc(stack_in[o][n % STACK], 16)

            def fv(b, half):
                sp.wait_ge(res_ready, 2 * b + half + 1)
                t = b * NT + 2 * half
                sp.dma_start(out.rearrange("(t p) d -> p t d", p=P)[:, t:t + 2, :],
                             x_sb[:, t:t + 2, :]).then_inc(res_out, 16)

            parts = {"qk_lo": qk_lo, "ld": ld, "fv": fv}
            for g, stages in steps:
                for name, b, args in stages:
                    if name in parts:
                        parts[name](b, *args)
            sp.wait_ge(res_out, 16 * 2 * B)


        @block.tensor
        def _(pe):
            def matmul3(dst, a_hi, a_lo, b_hi, b_lo, first, last):
                pe.matmul(dst, a_hi, b_hi, start=first, stop=False)
                pe.matmul(dst, a_lo, b_hi, start=False, stop=False)
                return pe.matmul(dst, a_hi, b_lo, start=False, stop=last)

            def scores(g):
                n, j = g // 8, g % 8
                m, par = j // 2, j % 2
                if j == 0:
                    pe.wait_ge(stack_in[0][n % STACK], 16 * (n // STACK + 1))
                    pe.wait_ge(stack_in[1][n % STACK], 16 * (n // STACK + 1))
                if g >= S_BANKS:
                    pe.wait_ge(exp_ready, g - S_BANKS + 1)
                rows = slice(64 * par, 64 * par + 64)
                pe.matmul(s_bank[g % S_BANKS][:, :], k_st[rows, n % STACK, m * P:(m + 1) * P],
                          q_st[rows, n % STACK, :], start=True, stop=True).then_inc(scores_ready, 1)

            def weigh(n):
                m, p = n % NT, (n // NT) % NP
                if m == 0 and n // NT >= AV_BANKS:
                    pe.wait_ge(ot_ready, n // NT - AV_BANKS + 1)
                pe.wait_ge(v_scaled, n + 1)
                for par in range(2):
                    mm = pe.matmul(av_bank[n // NT % AV_BANKS][64 * par:64 * par + 64, :], v_sb[:, m, 2 * p + par, :],
                                   e_sb[:, (2 * n + par) % E_RING, :], start=(m == 0), stop=(m == NT - 1))
                mm.then_inc(av_done, 1)

            def transposed(k):
                def t(b, half):
                    unit = (f"t{k}", b, (half,))
                    wait_bank(pe, unit)
                    i = k > 1
                    count = 2 * b + half if k == 1 else 4 * b + 2 * (k - 2) + half
                    pe.wait_ge(xn_ready[i], count + 1)
                    if unit == ("t1", 0, (0,)):
                        pe.wait_ge(id_in, 16)
                    for c in range(DC):
                        for t2 in range(2):
                            mm = pe.transpose(bank(unit)[:, c * HALF + t2 * P:c * HALF + (t2 + 1) * P],
                                              xn[i][:, t2, c * P:(c + 1) * P], id_sb[:, :])
                    mm.then_inc(filled[uses[unit][0]], 1)
                return t

            def qk(b, c, o):
                unit = ("qk", b, (c, o))
                wait_bank(pe, unit)
                for half in range(2):
                    wait_emptied(pe, ("t1", b, (half,)))
                if b == 0:
                    pe.wait_ge(wgt_lo, 1)
                cols = slice(o * D + c * P, o * D + (c + 1) * P)
                for d in range(DC):
                    mm = matmul3(bank(unit)[:, :], wqk_hi[:, d, cols], wqk_lo[:, d, cols],
                                 xt_hi[:, d, :], xt_lo[:, d, :], d == 0, d == DC - 1)
                mm.then_inc(filled[uses[unit][0]], 1)

            def v(b, hh, m):
                unit = ("v", b, (hh, m))
                wait_bank(pe, unit)
                wait_emptied(pe, ("t1", b, (m // 2,)))
                if b == 0:
                    pe.wait_ge(wgt_lo, 2)
                for d in range(DC):
                    mm = matmul3(bank(unit)[:, :], xt_hi[:, d, m * P:(m + 1) * P], xt_lo[:, d, m * P:(m + 1) * P],
                                 wv_hi[:, d, hh * 512:(hh + 1) * 512], wv_lo[:, d, hh * 512:(hh + 1) * 512],
                                 d == 0, d == DC - 1)
                mm.then_inc(filled[uses[unit][0]], 1)

            def op(b, hh, tt):
                unit = ("op", b, (hh, tt))
                wait_bank(pe, unit)
                pe.wait_ge(ot_ready, b * NP + 4 * hh + 4)
                if b == 0 and hh == 0:
                    pe.wait_ge(wgt_lo, 3)
                for t2 in range(2):
                    at = (2 * tt + t2) * P
                    for p in range(4):
                        mm = matmul3(bank(unit)[:, t2 * D:(t2 + 1) * D], ot_hi[:, p, at:at + P], ot_lo[:, p, at:at + P],
                                     wo_hi[:, 4 * hh + p, :], wo_lo[:, 4 * hh + p, :], p == 0, p == 3)
                mm.then_inc(filled[uses[unit][0]], 1)

            def kf_(b, gg):
                unit = ("kf", b, (gg,))
                wait_bank(pe, unit)
                pe.wait_ge(fm_ready, 1)
                pe.wait_ge(ctx_in, 16)
                for i in range(2):
                    mm = pe.matmul(bank(unit)[:, i * HALF:(i + 1) * HALF],
                                   fm_sb[:, i].rearrange("p h s e -> p (h s e)"), ctx_sb[:, gg, :],
                                   start=True, stop=True)
                mm.then_inc(filled[uses[unit][0]], 1)

            def kv(b):
                unit = ("kv", b, ())
                wait_bank(pe, unit)
                for gg in range(2):
                    wait_emptied(pe, ("kf", 0, (gg,)))
                for i in range(4):
                    mm = pe.transpose(bank(unit)[:, i * P:(i + 1) * P], kf[:, i, b].rearrange("p r l -> p (r l)"),
                                      id_sb[:, :])
                mm.then_inc(filled[uses[unit][0]], 1)

            def z(b, half, gg):
                unit = ("z", b, (half, gg))
                wait_bank(pe, unit)
                wait_emptied(pe, ("t2", b, (half,)))
                for i in range(2):
                    mm = pe.matmul(bank(unit)[:, i * HALF:(i + 1) * HALF],
                                   fm_sb[:, i].rearrange("p h s e -> p (h s e)"), xt2[:, gg, :],
                                   start=True, stop=True)
                mm.then_inc(filled[uses[unit][0]], 1)

            def xs(b, t, gg):
                unit = ("xs", b, (t, gg))
                wait_bank(pe, unit)
                wait_emptied(pe, ("z", b, (t // 2, gg)))
                if t == 0:
                    pe.wait_ge(kblk_ready, b + 1)
                for i in range(2):
                    mm = pe.matmul(bank(unit)[:, i * HALF:(i + 1) * HALF],
                                   qf[:, 2 * gg + i, (t % 2) * P:(t % 2 + 1) * P],
                                   kblk[:, 2 * gg + i].rearrange("p h l -> p (h l)"), start=True, stop=True)
                mm.then_inc(filled[uses[unit][0]], 1)

            def pt(b, t, gg):
                unit = ("pt", b, (t, gg))
                wait_bank(pe, unit)
                n = 8 * b + 2 * t + gg
                pe.wait_ge(xp_ready, n + 1)
                for i in range(4):
                    mm = pe.transpose(bank(unit)[:, i * P:(i + 1) * P], sx[:, n % 4, i * P:(i + 1) * P], id_sb[:, :])
                mm.then_inc(filled[uses[unit][0]], 1)

            def pv(b, half, gg):
                unit = ("pv", b, (half, gg))
                wait_bank(pe, unit)
                for t in (2 * half, 2 * half + 1):
                    wait_emptied(pe, ("pt", b, (t, gg)))
                wait_emptied(pe, ("kv", b, ()))
                for i in range(2):
                    for q in range(2):
                        pair = 4 * gg + 2 * i + q
                        mm = pe.matmul(bank(unit)[64 * q:64 * q + 64, i * HALF:(i + 1) * HALF], vblk[:, pair, :],
                                       pt_sb[:, pair, :], start=True, stop=True)
                mm.then_inc(filled[uses[unit][0]], 1)

            def fc(b, half):
                unit = ("fc", b, (half,))
                wait_bank(pe, unit)
                for gg in range(2):
                    wait_emptied(pe, ("pv", b, (half, gg)))
                if b == 0:
                    pe.wait_ge(post_in, 64)
                for t2 in range(2):
                    for i in range(4):
                        mm = pe.matmul(bank(unit)[:, t2 * D:(t2 + 1) * D], oxt[:, i, t2 * P:(t2 + 1) * P],
                                       wfc_sb[:, i, :], start=(i == 0), stop=(i == 3))
                mm.then_inc(filled[uses[unit][0]], 1)

            def fr(b, half):
                unit = ("fr", b, (half,))
                wait_bank(pe, unit)
                pe.wait_ge(mix_ready, 2 * b + half + 1)
                for t2 in range(2):
                    for c in range(DC):
                        mm = pe.matmul(bank(unit)[:, t2 * D:(t2 + 1) * D], mix_r[:, c, t2 * P:(t2 + 1) * P],
                                       wffn_sb[:, 0, c, :], start=(c == 0), stop=(c == DC - 1))
                mm.then_inc(filled[uses[unit][0]], 1)

            def fk(b, half):
                unit = ("fk", b, (half,))
                wait_bank(pe, unit)
                pe.wait_ge(mix_ready, 2 * b + half + 1)
                for mc in range(DC):
                    for c in range(DC):
                        mm = pe.matmul(bank(unit)[:, mc * HALF:(mc + 1) * HALF],
                                       wffn_sb[:, 1, c, mc * P:(mc + 1) * P], mix_k[:, c, :],
                                       start=(c == 0), stop=(c == DC - 1))
                mm.then_inc(filled[uses[unit][0]], 1)

            def fv(b, half):
                unit = ("fv", b, (half,))
                wait_bank(pe, unit)
                pe.wait_ge(kact_ready, 2 * b + half + 1)
                for t2 in range(2):
                    for c in range(DC):
                        mm = pe.matmul(bank(unit)[:, t2 * D:(t2 + 1) * D], kact[:, c, t2 * P:(t2 + 1) * P],
                                       wffn_sb[:, 2, c, :], start=(c == 0), stop=(c == DC - 1))
                mm.then_inc(filled[uses[unit][0]], 1)

            parts = {"t1": transposed(1), "t2": transposed(2), "t3": transposed(3), "qk": qk, "v": v, "op": op,
                     "kf": kf_, "kv": kv, "z": z, "xs": xs, "pt": pt, "pv": pv, "fc": fc, "fr": fr, "fk": fk, "fv": fv}
            for g, stages in steps:
                if 0 <= g < TILES:
                    scores(g)
                _, n, _ = lagged(g)
                if n is not None:
                    weigh(n)
                for name, b, args in stages:
                    if name in parts:
                        parts[name](b, *args)

        @block.scalar
        def _(act):
            def exponentials(g):
                act.wait_ge(nmax_ready, g + 1)
                if g >= E_RING:
                    act.wait_ge(av_done, (g - E_RING) // 2 + 1)
                act.activation(e_sb[:, g % E_RING, :], s_bank[g % S_BANKS][:, :], ACT.Exp,
                               bias=nmax[:, g % E_RING:g % E_RING + 1],
                               accum_out=esum[:, g % (2 * E_RING):g % (2 * E_RING) + 1]).then_inc(exp_ready, 1)

            def ot_high(n):
                act.wait_ge(av_done, NT * (n + 1))
                if n >= 4:
                    last = (n // 4 - 1)
                    wait_filled(act, ("op", last // 2, (last % 2, 1)))
                act.activation(ot_hi[:, n % 4, :], av_bank[n % AV_BANKS][:, :], ACT.Copy).then_inc(ot_hi_ready, 1)

            def cut(b, which):
                if which == "qk":
                    act.wait_ge(wqk_in, 16)
                    act.activation(wqk_hi[:, :, 0:D], wqk_raw[:, :, 0:D], ACT.Copy, scale=KD ** -0.5)
                    act.activation(wqk_hi[:, :, D:], wqk_raw[:, :, D:], ACT.Copy).then_inc(wgt_hi, 1)
                elif which == "v":
                    act.wait_ge(wv_in, 16)
                    act.activation(wv_hi[:, :, :], wv_raw, ACT.Copy).then_inc(wgt_hi, 1)
                else:
                    act.wait_ge(wo_in, 16)
                    act.activation(wo_hi[:, :, :], wo_raw[:, :, :], ACT.Copy).then_inc(wgt_hi, 1)

            def t1(b, half):
                unit = ("t1", b, (half,))
                wait_filled(act, unit)
                if b:
                    wait_filled(act, ("v", b - 1, (1, NT - 1)))
                    wait_filled(act, ("qk", b - 1, (1, 1)))
                act.activation(xt_hi[:, :, half * HALF:(half + 1) * HALF],
                               bank(unit)[:, :].rearrange("p (c n) -> p c n", c=DC), ACT.Copy).then_inc(xt_hi_ready, 1)

            def qk(b, c, o):
                unit = ("qk", b, (c, o))
                wait_filled(act, unit)
                n = 2 * b + c
                if n:
                    act.wait_ge(stack_out[o][(n - 1) % 2], 64 * ((n - 1) // 2 + 1))
                act.activation(qkt_hi[:, o, :], bank(unit)[:, :], ACT.Copy).then_inc(qk_hi_ready, 1)

            def v(b, hh, m):
                if m % 2 == 0:
                    unit = ("v", b, (hh, m))
                    wait_filled(act, unit)
                    if b:
                        act.wait_ge(av_done, NT * ((b - 1) * NP + 4 * hh + 4))
                    act.activation(v_sb[:, m, 8 * hh:8 * hh + 8, :],
                                   bank(unit)[:, :].rearrange("p (h v) -> p h v", h=8), ACT.Copy)\
                       .then_inc(emptied[uses[unit][0]], 1)

            def kf_(b, gg):
                unit = ("kf", b, (gg,))
                wait_filled(act, unit)
                for twice in range(2):
                    for i in range(2):
                        ins = act.activation(kf[:, 2 * gg + i, :, twice, :],
                                             bank(unit)[:, i * HALF:(i + 1) * HALF].rearrange("p (b l) -> p b l", b=B),
                                             ACT.Exp, bias=fmb[:, 0:1])
                ins.then_inc(emptied[uses[unit][0]], 1)

            def t2(b, half):
                unit = ("t2", b, (half,))
                wait_filled(act, unit)
                if (b, half) != (0, 0):
                    pb, ph = (b, 0) if half else (b - 1, 1)
                    wait_filled(act, ("z", pb, (ph, 1)))
                act.activation(xt2[:, :, :], bank(unit)[:, :].rearrange("p (c n) -> p c n", c=DC), ACT.Copy)\
                   .then_inc(emptied[uses[unit][0]], 1)

            def z(b, half, gg):
                unit = ("z", b, (half, gg))
                wait_filled(act, unit)
                if (b, half) != (0, 0):
                    pb, ph = (b, 0) if half else (b - 1, 1)
                    wait_filled(act, ("xs", pb, (2 * ph + 1, gg)))
                act.activation(qf[:, 2 * gg:2 * gg + 2, :], bank(unit)[:, :].rearrange("p (g n) -> p g n", g=2),
                               ACT.Exp, bias=fmb[:, 0:1]).then_inc(emptied[uses[unit][0]], 1)

            def xs(b, t, gg):
                n = 8 * b + 2 * t + gg
                wait_emptied(act, ("xs", b, (t, gg)))
                act.activation(sx[:, n % 4, :], sx[:, n % 4, :], ACT.Exp).then_inc(xexp_ready, 1)

            def pt(b, t, gg):
                unit = ("pt", b, (t, gg))
                wait_filled(act, unit)
                if (b, t) >= (0, 2):
                    pb, ph = (b, 0) if t >= 2 else (b - 1, 1)
                    wait_filled(act, ("pv", pb, (ph, gg)))
                act.activation(pt_sb[:, 4 * gg:4 * gg + 4, (t % 2) * P:(t % 2 + 1) * P],
                               bank(unit)[:, :].rearrange("p (i n) -> p i n", i=4), ACT.Copy)\
                   .then_inc(emptied[uses[unit][0]], 1)

            def pv(b, half, gg):
                unit = ("pv", b, (half, gg))
                wait_filled(act, unit)
                if (b, half) != (0, 0):
                    pb, ph = (b, 0) if half else (b - 1, 1)
                    wait_filled(act, ("fc", pb, (ph,)))
                act.activation(oxt[:, 2 * gg:2 * gg + 2, :], bank(unit)[:, :].rearrange("p (i n) -> p i n", i=2),
                               ACT.Copy).then_inc(emptied[uses[unit][0]], 1)

            def t3(b, half):
                unit = ("t3", b, (half,))
                wait_filled(act, unit)
                if b and half == 0:
                    act.wait_ge(mix_ready, 2 * b)
                act.activation(xt3[:, :, 1 + half * HALF:1 + (half + 1) * HALF],
                               bank(unit)[:, :].rearrange("p (c n) -> p c n", c=DC), ACT.Copy)\
                   .then_inc(emptied[uses[unit][0]], 1)

            def fr(b, half):
                unit = ("fr", b, (half,))
                wait_filled(act, unit)
                n = 2 * b + half
                if n:
                    act.wait_ge(res_ready, n)
                act.activation(gate[:, :, :], bank(unit)[:, :].rearrange("p (t d) -> p t d", t=2), ACT.Tanh,
                               scale=0.5).then_inc(emptied[uses[unit][0]], 1)

            def fk(b, half):
                unit = ("fk", b, (half,))
                wait_filled(act, unit)
                if (b, half) != (0, 0):
                    pb, ph = (b, 0) if half else (b - 1, 1)
                    wait_filled(act, ("fv", pb, (ph,)))
                act.activation(kact[:, :, :], bank(unit)[:, :].rearrange("p (c n) -> p c n", c=DC), ACT.Relu)\
                   .then_inc(emptied[uses[unit][0]], 1)

            parts = {"cut": cut, "t1": t1, "qk": qk, "v": v, "kf": kf_, "t2": t2, "z": z, "xs": xs, "pt": pt,
                     "pv": pv, "t3": t3, "fr": fr, "fk": fk}
            for g, stages in steps:
                _, _, n = lagged(g)
                if n is not None:
                    ot_high(n)
                if 0 <= g < TILES:
                    exponentials(g)
                for name, b, args in stages:
                    if name in parts:
                        parts[name](b, *args)

        @block.vector
        def _(dve):
            chained = [0]

            def link(ins):
                chained[0] += 1
                ins.then_inc(dve_chain, 1)
                dve.wait_ge(dve_chain, chained[0])

            dve.memset(vblk[:, :, :], 0.0).then_inc(consts_set, 1)

            def maxima(g):
                dve.wait_ge(scores_ready, g + 1)
                dve.tensor_reduce(nmax[:, g % E_RING:g % E_RING + 1], s_bank[g % S_BANKS][:, :], AX_X, ALU.max,
                                  negate=True).then_inc(nmax_ready, 1)

            def row_sums(n):
                dve.wait_ge(exp_ready, 2 * n + 2)
                at = (2 * n) % (2 * E_RING)
                if n >= 4:
                    dve.wait_ge(v_scaled, n - 3)
                dve.reciprocal(rsum[:, n % 4, :], esum[:, at:at + 2]).then_inc(rsum_ready, 1)

            def ot_low(n):
                dve.wait_ge(ot_hi_ready, n + 1)
                dve.tensor_tensor(ot_lo[:, n % 4, :], av_bank[n % AV_BANKS][:, :], ot_hi[:, n % 4, :].bitcast(F32), ALU.subtract)\
                   .then_inc(ot_ready, 1)

            def cut(b, which):
                if which == "qk":
                    dve.wait_ge(wgt_hi, 1)
                    dve.scalar_tensor_tensor(out=wqk_lo[:, :, 0:D], in0=wqk_raw[:, :, 0:D], scalar=KD ** -0.5,
                                             in1=wqk_hi[:, :, 0:D].bitcast(F32), op0=ALU.mult, op1=ALU.subtract)
                    dve.tensor_tensor(wqk_lo[:, :, D:], wqk_raw[:, :, D:], wqk_hi[:, :, D:].bitcast(F32),
                                      ALU.subtract).then_inc(wgt_lo, 1)
                elif which == "v":
                    dve.wait_ge(wgt_hi, 2)
                    dve.tensor_tensor(wv_lo[:, :, :], wv_raw, wv_hi[:, :, :].bitcast(F32), ALU.subtract)\
                       .then_inc(wgt_lo, 1)
                else:
                    dve.wait_ge(wgt_hi, 3)
                    dve.tensor_tensor(wo_lo[:, :, :], wo_raw[:, :, :], wo_hi[:, :, :].bitcast(F32), ALU.subtract)\
                       .then_inc(wgt_lo, 1)

            def norm_stats(k):
                def ln(b, half):
                    i = k > 1
                    count = 2 * b + half if k == 1 else 4 * b + 2 * (k - 2) + half
                    if k == 1:
                        dve.wait_ge(x_in[b], 16)
                    elif k == 2:
                        wait_emptied(dve, ("op", b, (1, half)))
                    else:
                        wait_emptied(dve, ("fc", b, (half,)))
                    if count:
                        dve.wait_ge(xn_ready[i], count)
                    for t2 in range(2):
                        ins = dve.bn_stats(stats[i][:, t2, :], x_sb[:, b * NT + 2 * half + t2, :])
                    link(ins)
                    for t2 in range(2):
                        ins = dve.bn_aggr(mv[i][:, t2, :], stats[i][:, t2, :])
                    link(ins)
                    dve.tensor_scalar(nmean[i][:, :], mv[i][:, :, 0], -1.0, None, ALU.mult)
                    dve.tensor_scalar(veps[i][:, :], mv[i][:, :, 1], EPS, None, ALU.add).then_inc(var_ready[i], 1)
                return ln

            def t1_lo(b, half):
                unit = ("t1", b, (half,))
                dve.wait_ge(xt_hi_ready, 2 * b + half + 1)
                at = slice(half * HALF, (half + 1) * HALF)
                dve.tensor_tensor(xt_lo[:, :, at], bank(unit)[:, :].rearrange("p (c n) -> p c n", c=DC),
                                  xt_hi[:, :, at].bitcast(F32), ALU.subtract).then_inc(emptied[uses[unit][0]], 1)

            def qk_lo(b, c, o):
                unit = ("qk", b, (c, o))
                dve.wait_ge(qk_hi_ready, 4 * b + 2 * c + o + 1)
                dve.tensor_tensor(qkt_lo[:, o, :], bank(unit)[:, :], qkt_hi[:, o, :].bitcast(F32), ALU.subtract)\
                   .then_inc(emptied[uses[unit][0]], 1)

            def v(b, hh, m):
                if m % 2:
                    unit = ("v", b, (hh, m))
                    wait_filled(dve, unit)
                    if b:
                        dve.wait_ge(av_done, NT * ((b - 1) * NP + 4 * hh + 4))
                    dve.tensor_copy(v_sb[:, m, 8 * hh:8 * hh + 8, :],
                                    bank(unit)[:, :].rearrange("p (h v) -> p h v", h=8))\
                       .then_inc(emptied[uses[unit][0]], 1)

            def op(b, hh, tt):
                unit = ("op", b, (hh, tt))
                wait_filled(dve, unit)
                at = b * NT + 2 * tt
                if hh:
                    wait_emptied(dve, ("op", b, (0, tt)))
                dve.tensor_tensor(x_sb[:, at:at + 2, :], bank(unit)[:, :].rearrange("p (t d) -> p t d", t=2),
                                  x_sb[:, at:at + 2, :], ALU.add).then_inc(emptied[uses[unit][0]], 1)

            def feat(b):
                dve.wait_ge(fm_in, 16 * 25)
                dve.tensor_scalar(fm_sb[:, :, :, 1, :].rearrange("p g h e -> p (g h) e"),
                                  fm_sb[:, :, :, 1, :].rearrange("p g h e -> p (g h) e"), -1.0, None, ALU.mult)
                dve.tensor_tensor(fmb[:, :], fmb[:, :], sign_sb[:, :], ALU.mult).then_inc(fm_ready, 1)

            def kv(b):
                unit = ("kv", b, ())
                wait_filled(dve, unit)
                if b:
                    wait_filled(dve, ("xs", b - 1, (NT - 1, 0)))
                    wait_filled(dve, ("xs", b - 1, (NT - 1, 1)))
                else:
                    dve.wait_ge(consts_set, 2)
                for h in range(4):
                    ins = dve.tensor_scalar(kblk[32 * h:32 * h + 32, :, h, :], kf[32 * h:32 * h + 32, :, b, 0, :],
                                            D ** -0.5, None, ALU.mult)
                ins.then_inc(kblk_ready, 1)
                if b:
                    wait_filled(dve, ("pv", b - 1, (1, 1)))
                v4 = bank(unit)[:, :].rearrange("p (r q s) -> p r q s", q=2, s=FE)
                for q in range(2):
                    ins = dve.tensor_copy(vblk[64 * q:64 * q + 64, :, q * FE:(q + 1) * FE],
                                          v4[64 * q:64 * q + 64, :, q, :])
                ins.then_inc(emptied[uses[unit][0]], 1)

            def xs(b, t, gg):
                unit = ("xs", b, (t, gg))
                wait_filled(dve, unit)
                n = 8 * b + 2 * t + gg
                src = bank(unit)[:, :].rearrange("p (h l) -> p h l", h=8)
                link(dve.tensor_reduce(xmax[:, n % 4, :], src, AX_X, ALU.max, negate=True))
                if n >= 4:
                    pb, r = (n - 4) // 8, (n - 4) % 8
                    wait_filled(dve, ("pt", pb, (r // 2, r % 2)))
                dve.tensor_tensor(sx[:, n % 4, :].rearrange("p (h l) -> p h l", h=8), src,
                                  xmax[:, n % 4, :].unsqueeze(2).broadcast_to([P, 8, L]), ALU.add)\
                   .then_inc(emptied[uses[unit][0]], 1)

            def xn_(b, t, gg):
                n = 8 * b + 2 * t + gg
                dve.wait_ge(xexp_ready, n + 1)
                link(dve.tensor_reduce(xsum[:, n % 4, :], sx[:, n % 4, :].rearrange("p (h l) -> p h l", h=8),
                                       AX_X, ALU.add))
                if n >= 4:
                    dve.wait_ge(xp_ready, n - 3)
                dve.reciprocal(xrec[:, n % 4, :], xsum[:, n % 4, :]).then_inc(xrec_ready, 1)

            def fc(b, half):
                unit = ("fc", b, (half,))
                wait_filled(dve, unit)
                dve.wait_ge(bias_added, 2 * b + half + 1)
                at = b * NT + 2 * half
                dve.tensor_tensor(x_sb[:, at:at + 2, :], bank(unit)[:, :].rearrange("p (t d) -> p t d", t=2),
                                  x_sb[:, at:at + 2, :], ALU.add).then_inc(emptied[uses[unit][0]], 1)

            def mix(b, half):
                wait_emptied(dve, ("t3", b, (half,)))
                n = 2 * b + half
                if n == 0:
                    dve.wait_ge(post_in, 64)
                if n:
                    pb, ph = (b, 0) if half else (b - 1, 1)
                    wait_filled(dve, ("fr", pb, (ph,)))
                    wait_filled(dve, ("fk", pb, (ph,)))
                cur = xt3[:, :, 1 + half * HALF:1 + (half + 1) * HALF]
                prev = xt3[:, :, half * HALF:(half + 1) * HALF]
                link(dve.tensor_tensor(mix_k[:, :, :], cur, prev, ALU.subtract))
                for c in range(DC):
                    ins = dve.scalar_tensor_tensor(out=mix_r[:, c, :], in0=mix_k[:, c, :], scalar=mu_sb[:, 0, c:c + 1],
                                                   in1=prev[:, c, :], op0=ALU.mult, op1=ALU.add)
                link(ins)
                for c in range(DC):
                    ins = dve.scalar_tensor_tensor(out=mix_k[:, c, :], in0=mix_k[:, c, :], scalar=mu_sb[:, 1, c:c + 1],
                                                   in1=prev[:, c, :], op0=ALU.mult, op1=ALU.add)
                ins.then_inc(mix_ready, 1)

            def fv(b, half):
                unit = ("fv", b, (half,))
                wait_filled(dve, unit)
                wait_emptied(dve, ("fr", b, (half,)))
                at = b * NT + 2 * half
                dve.scalar_tensor_tensor(out=gate[:, :, :], in0=gate[:, :, :], scalar=1.0,
                                         in1=bank(unit)[:, :].rearrange("p (t d) -> p t d", t=2),
                                         op0=ALU.add, op1=ALU.mult).then_inc(emptied[uses[unit][0]], 1)
                wait_emptied(dve, unit)
                dve.scalar_tensor_tensor(out=x_sb[:, at:at + 2, :], in0=gate[:, :, :], scalar=0.5,
                                         in1=x_sb[:, at:at + 2, :], op0=ALU.mult, op1=ALU.add).then_inc(res_ready, 1)

            parts = {"cut": cut, "ln1": norm_stats(1), "ln2": norm_stats(2), "ln3": norm_stats(3), "t1_lo": t1_lo,
                     "qk_lo": qk_lo, "v": v, "op": op, "feat": feat, "kv": kv, "xs": xs, "xn": xn_, "fc": fc,
                     "mix": mix, "fv": fv}
            for g, stages in steps:
                n, _, pair = lagged(g)
                if pair is not None:
                    ot_low(pair)
                if 0 <= g < TILES:
                    maxima(g)
                if n is not None:
                    row_sums(n)
                for name, b, args in stages:
                    if name in parts:
                        parts[name](b, *args)

        @block.gpsimd
        def _(pool):
            pool.memset(fm_sb[:, :, :, :, :], 0.0).then_inc(fm_zero, 1)
            pool.memset(power[:, :], -0.5).then_inc(pool_chain, 1)
            pool.memset(kblk[:, :, :, :], 0.0).then_inc(pool_chain, 1)
            pool.memset(xt3[:, :, 0:1], 0.0).then_inc(consts_set, 1)
            pool.wait_ge(pool_chain, 2)

            def scale_values(n):
                m, p = n % NT, (n // NT) % NP
                pool.wait_ge(rsum_ready, n + 1)
                if p % 4 == 0:
                    wait_emptied(pool, ("v", n // (NT * NP), (p // 4, m)))
                pool.tensor_tensor(v_sb[:, m, 2 * p:2 * p + 2, :], v_sb[:, m, 2 * p:2 * p + 2, :],
                                   rsum[:, n % 4, :].unsqueeze(2).broadcast_to([P, 2, VD]), ALU.mult)\
                    .then_inc(v_scaled, 1)

            def norm_apply(k):
                def ln(b, half):
                    i = k > 1
                    count = 2 * b + half if k == 1 else 4 * b + 2 * (k - 2) + half
                    pool.wait_ge(var_ready[i], count + 1)
                    pool.tensor_tensor(rstd[i][:, :], veps[i][:, :], power[:, :], ALU.pow).then_inc(rstd_ready[i], 1)
                    pool.wait_ge(rstd_ready[i], count + 1)
                    if k == 1 and count:
                        pb, ph = (b, 0) if half else (b - 1, 1)
                        wait_filled(pool, ("t1", pb, (ph,)))
                    elif k > 1 and count:
                        pk, pb, ph = (k, b, 0) if half else (2, b, 1) if k == 3 else (3, b - 1, 1)
                        wait_filled(pool, (f"t{pk}", pb, (ph,)))
                    for t2 in range(2):
                        ins = pool.tensor_scalar(xn[i][:, t2, :], x_sb[:, b * NT + 2 * half + t2, :],
                                                 nmean[i][:, t2:t2 + 1], rstd[i][:, t2:t2 + 1], ALU.add, ALU.mult)
                    ins.then_inc(xn_ready[i], 1)
                    if k == 2:
                        pool.wait_ge(xn_ready[i], count + 1)
                        if count == 0:
                            pool.wait_ge(post_in, 64)
                        at = b * NT + 2 * half
                        pool.tensor_tensor(x_sb[:, at:at + 2, :], x_sb[:, at:at + 2, :],
                                           fcb[:, :].unsqueeze(1).broadcast_to([P, 2, D]), ALU.add)\
                            .then_inc(bias_added, 1)
                return ln

            def xn_(b, t, gg):
                n = 8 * b + 2 * t + gg
                pool.wait_ge(xrec_ready, n + 1)
                sx3 = sx[:, n % 4, :].rearrange("p (h l) -> p h l", h=8)
                pool.tensor_tensor(sx3, sx3, xrec[:, n % 4, :].unsqueeze(2).broadcast_to([P, 8, L]), ALU.mult)\
                    .then_inc(xp_ready, 1)

            def fk(b, half):
                wait_emptied(pool, ("fk", b, (half,)))
                pool.tensor_tensor(kact[:, :, :], kact[:, :, :], kact[:, :, :], ALU.mult).then_inc(kact_ready, 1)

            parts = {"ln1": norm_apply(1), "ln2": norm_apply(2), "ln3": norm_apply(3), "xn": xn_, "fk": fk}
            for g, stages in steps:
                n, _, _ = lagged(g)
                if n is not None:
                    scale_values(n)
                for name, b, args in stages:
                    if name in parts:
                        parts[name](b, *args)


def kernel(x, ctx_1024, L0_attn_query_proj, L0_attn_key_proj, L0_attn_value_proj, L0_attn_output_proj,
           L0_xattn_fm_w, L0_xattn_fm_b, L0_xattn_fc_w, L0_xattn_fc_b, L0_ffn_W_r, L0_ffn_W_k, L0_ffn_W_v,
           L0_ffn_mu_r, L0_ffn_mu_k):
    import numpy as np
    import concourse.bacc as bacc
    from concourse.bass_utils import run_bass_kernel_spmd

    def rows(a, c):
        return np.ascontiguousarray(np.reshape(a, (c, P, -1)).transpose(1, 0, 2))

    wq = np.asarray(L0_attn_query_proj).transpose(2, 1, 0).reshape(D, H * KD)
    wk = np.asarray(L0_attn_key_proj).transpose(2, 0, 1).reshape(D, H * KD)
    arrays = {
        "x": np.asarray(x).reshape(B * N, D),
        "ctx_t": rows(np.asarray(ctx_1024).transpose(2, 0, 1).reshape(D, B * L), DC),
        "wqk": rows(np.concatenate([wq, wk], axis=1), DC),
        "wv": rows(np.asarray(L0_attn_value_proj).transpose(2, 0, 1).reshape(D, H * VD), DC),
        "wo": rows(np.asarray(L0_attn_output_proj).transpose(1, 2, 0).reshape(H * VD, D), NP),
        "fm_t": np.ascontiguousarray(np.asarray(L0_xattn_fm_w).T),
        "fm_b": np.asarray(L0_xattn_fm_b).reshape(KD, 1),
        "wfc": rows(np.asarray(L0_xattn_fc_w).T, 4),
        "fc_b": np.asarray(L0_xattn_fc_b),
        "wffn": np.ascontiguousarray(np.stack([rows(np.asarray(w).T, DC) for w in (L0_ffn_W_r, L0_ffn_W_k, L0_ffn_W_v)], axis=1)),
        "mu": np.ascontiguousarray(np.stack([np.asarray(m).reshape(DC, P).T for m in (L0_ffn_mu_r, L0_ffn_mu_k)], axis=1)),
        "ident": np.eye(P, dtype=np.float32),
        "sign": np.tile(np.repeat(np.array([1.0, -1.0], np.float32), KD), 4).reshape(P, 1),
    }
    nc = bacc.Bacc("TRN2", target_bir_lowering=False, num_devices=1)
    aps = {k: nc.dram_tensor(f"in_{k}", a.shape, mybir.dt.from_np(a.dtype), kind="ExternalInput").ap()
           for k, a in arrays.items()}
    aps["out"] = nc.dram_tensor("out", (B * N, D), F32, kind="ExternalOutput").ap()
    build(nc, **aps)
    r = run_bass_kernel_spmd(nc, [{f"in_{k}": a for k, a in arrays.items()}], core_ids=[0])
    return r.results[0]["out"].reshape(B, N, D)
```

```python
from contextlib import ExitStack

import concourse.bass as bass
from concourse import mybir

F32 = mybir.dt.float32
F32R = mybir.dt.float32r
ALU = mybir.AluOpType
ACT = mybir.ActivationFunctionType
AX_X = mybir.AxisListType.X

P = 128
B, N, D = 4, 512, 256
H, KD, VD = 16, 16, 64
L, FE = 64, 32
EPS = 1e-5
DC = D // P
NT = N // P
NP = H // 2
HALF = N // 2
STEPS = NP * NT * 2
TILES = B * STEPS
S_BANKS, AV_BANKS, MISC_BANKS = 3, 2, 3
E_RING = 8
X_RING = 3
STACK = 4
AV_LAG, SCALE_LAG = 6, 2
OE_LAG = 2 * NT + AV_LAG - 1

X_TILES = 3
BANKED = {"t1", "qk", "v", "op", "t2", "kv", "kf", "z", "xs", "pt", "pv", "fc", "t3", "fr", "fk", "fv"}

PLAN = [
    (1, "qk", 0, (1, 0)), (2, "qk_lo", 0, (1, 0)), (5, "qk", 0, (1, 1)), (5, "qk_lo", 0, (1, 1)), (6, "v", 0, (1, 0)),
    (6, "kv", -1, ()), (8, "ld", 0, (3,)), (8, "op", -1, (1, 0)), (9, "v", 0, (1, 1)), (9, "ln2", -1, (0,)),
    (11, "op", -1, (1, 1)), (12, "ln2", -1, (1,)), (12, "t2", -1, (0,)), (12, "t2_lo", -1, (0,)),
    (13, "v", 0, (1, 2)), (14, "z", -1, (0, 0)), (15, "z", -1, (0, 1)), (16, "t2", -1, (1,)), (16, "xs", -1, (0, 0)),
    (16, "t2_lo", -1, (1,)), (17, "ld", 0, (4,)), (17, "v", 0, (1, 3)), (17, "xs", -1, (0, 1)),
    (19, "xn", -1, (0, 0)), (19, "z", -1, (1, 0)), (19, "xs", -1, (1, 0)), (20, "xn", -1, (0, 1)),
    (21, "xn", -1, (1, 0)), (21, "pt", -1, (0, 0)), (22, "ld", 0, (5,)), (22, "xs", -1, (1, 1)),
    (24, "xn", -1, (1, 1)), (24, "z", -1, (1, 1)), (25, "pt", -1, (0, 1)), (25, "pt", -1, (1, 0)),
    (26, "xs", -1, (2, 0)), (26, "xs", -1, (2, 1)), (27, "pt", -1, (1, 1)), (27, "xn", -1, (2, 0)),
    (27, "xs", -1, (3, 0)), (28, "pv", -1, (0, 0)), (28, "xn", -1, (2, 1)), (28, "pv", -1, (0, 1)),
    (28, "pv_lo", -1, (0, 0)), (28, "pv_lo", -1, (0, 1)), (29, "xn", -1, (3, 0)), (29, "pt", -1, (2, 0)),
    (29, "xs", -1, (3, 1)), (30, "xn", -1, (3, 1)), (30, "fc", -1, (0,)), (31, "ln3", -1, (0,)),
    (31, "pt", -1, (2, 1)), (32, "pt", -1, (3, 0)), (33, "ln1", 1, (0,)), (33, "pt", -1, (3, 1)),
    (35, "pv", -1, (1, 0)), (36, "ld", 0, (6,)), (36, "t3", -1, (0,)), (36, "pv", -1, (1, 1)),
    (36, "pv_lo", -1, (1, 0)), (36, "pv_lo", -1, (1, 1)), (38, "t1", 1, (0,)), (38, "ln1", 1, (1,)),
    (38, "mix", -1, (0,)), (38, "fc", -1, (1,)), (39, "ln3", -1, (1,)), (39, "t1_lo", 1, (0,)),
    (40, "t1_lo", 1, (1,)), (40, "op", 0, (0, 0)), (40, "t1", 1, (1,)), (41, "fk", -1, (0,)), (42, "t3", -1, (1,)),
    (43, "ld", 0, (7,)), (43, "fr", -1, (0,)), (43, "qk", 1, (0, 0)), (43, "mix", -1, (1,)), (44, "qk_lo", 1, (0, 0)),
    (44, "op", 0, (0, 1)), (47, "qk", 1, (0, 1)), (47, "qk_lo", 1, (0, 1)), (47, "v", 1, (0, 0)),
    (49, "fv", -1, (0,)), (51, "fk", -1, (1,)), (52, "v", 1, (0, 1)), (53, "fr", -1, (1,)), (55, "fv", -1, (1,)),
    (55, "v", 1, (0, 2)), (58, "ld", 1, (0,)), (61, "ld", 1, (1,)), (63, "v", 1, (0, 3)), (63, "x_load", 2, ()),
    (63, "ld", 1, (2,)),
]
LAST = [
    (6, "kv", ()), (8, "op", (1, 0)), (8, "ln2", (0,)), (12, "op", (1, 1)), (12, "ln2", (1,)), (14, "t2", (0,)),
    (14, "t2_lo", (0,)), (15, "z", (0, 0)), (16, "z", (0, 1)), (16, "t2_lo", (1,)), (17, "t2", (1,)),
    (17, "xs", (0, 0)), (17, "xs", (0, 1)), (18, "xn", (0, 0)), (18, "xs", (1, 0)), (19, "xn", (0, 1)),
    (19, "xs", (1, 1)), (19, "pt", (0, 0)), (20, "xn", (1, 0)), (20, "z", (1, 0)), (20, "z", (1, 1)),
    (21, "pt", (0, 1)), (21, "xn", (1, 1)), (21, "pt", (1, 0)), (22, "xs", (2, 0)), (22, "pt", (1, 1)),
    (23, "xs", (2, 1)), (25, "xn", (2, 0)), (25, "xn", (2, 1)), (25, "pv", (0, 0)), (25, "pv", (0, 1)),
    (26, "pv_lo", (0, 0)), (26, "xs", (3, 0)), (27, "pv_lo", (0, 1)), (29, "xs", (3, 1)), (30, "xn", (3, 0)),
    (30, "xn", (3, 1)), (30, "pt", (2, 0)), (30, "fc", (0,)), (31, "ln3", (0,)), (32, "mix", (0,)),
    (32, "pt", (2, 1)), (33, "pv_lo", (1, 0)), (33, "pt", (3, 0)), (33, "pt", (3, 1)), (34, "t3", (0,)),
    (34, "pv", (1, 0)), (35, "pv", (1, 1)), (35, "pv_lo", (1, 1)), (35, "fc", (1,)), (36, "fr", (0,)),
    (38, "ln3", (1,)), (40, "fk", (0,)), (42, "t3", (1,)), (42, "mix", (1,)), (44, "fv", (0,)), (51, "fk", (1,)),
    (54, "fr", (1,)), (63, "fv", (1,)),
]
FIRST = [
    ("t1", 0, (0,)), ("ln1", 0, (0,)), ("ln1", 0, (1,)), ("cut", 0, ("qk",)), ("t1_lo", 0, (0,)), ("t1_lo", 0, (1,)),
    ("t1", 0, (1,)), ("cut", 0, ("v",)), ("qk", 0, (0, 0)), ("qk_lo", 0, (0, 0)), ("qk_lo", 0, (0, 1)),
    ("load", 0, ("fc",)), ("ld", 0, (0,)), ("qk", 0, (0, 1)), ("load", 0, ("o",)), ("ld", 0, (1,)), ("v", 0, (0, 0)),
    ("load", 0, ("rest",)), ("ld", 0, (2,)), ("load", 0, ("feat",)), ("v", 0, (0, 1)), ("v", 0, (0, 2)),
    ("v", 0, (0, 3)),
]
ONCE = [
    (1, "cut", ("fc",)), (1, "cut", ("o",)), (5, "feat", ()), (14, "kf", (0,)), (15, "kf", (1,)),
]


def schedule():
    rounds = [(-1, FIRST)]
    for r in range(B + 1):
        for step in range(STEPS):
            plan = PLAN if r < B else [(at, name, -1, args) for at, name, args in LAST]
            stages = [(name, 0, args) for at, name, args in ONCE if (r, step) == (0, at)]
            stages += [(name, r + off, args) for at, name, off, args in plan if at == step and 0 <= r + off < B]
            rounds.append((r * STEPS + step, stages))
    return rounds


def bank_uses(steps):
    uses, had = {}, [0] * (MISC_BANKS + S_BANKS)
    n = 0
    for g, stages in steps:
        ring = MISC_BANKS if 0 <= g < TILES else MISC_BANKS + S_BANKS
        for unit in stages:
            if unit[0] in BANKED:
                uses[unit] = (n % ring, had[n % ring])
                had[n % ring] += 1
                n += 1
    return uses


def banks_before_scores(steps, uses):
    units = [unit for g, stages in steps if g < 0 for unit in stages if unit[0] in BANKED]
    return [sum(uses[u][0] == MISC_BANKS + i for u in units) for i in range(S_BANKS)]


def build(nc, x, ctx_t, wqk, wv, wo, fm_t, fm_b, wfc, fc_b, wffn, mu, ident, sign, out):
    steps = schedule()
    uses = bank_uses(steps)
    used_before = banks_before_scores(steps, uses)

    with ExitStack() as ctx:
        def sb(name, shape, dt=F32):
            return ctx.enter_context(nc.sbuf_tensor(name, shape, dt))

        def sem(name):
            return ctx.enter_context(nc.semaphore(name))

        x_sb = sb("x_sb", [P, X_RING * NT, D])
        wqk_hi, wqk_lo = sb("wqk_hi", [P, DC, 2 * H * KD], F32R), sb("wqk_lo", [P, DC, 2 * H * KD], F32R)
        wv_hi, wv_lo = sb("wv_hi", [P, DC, H * VD], F32R), sb("wv_lo", [P, DC, H * VD], F32R)
        wo_hi, wo_lo = sb("wo_hi", [P, NP, D], F32R), sb("wo_lo", [P, NP, D], F32R)
        wfc_hi, wfc_lo = sb("wfc_hi", [P, 4, D], F32R), sb("wfc_lo", [P, 4, D], F32R)
        wffn_sb = sb("wffn_sb", [P, 3, DC, D])
        fm_sb = sb("fm_sb", [P, 2, 4, 2, KD])
        fm_hi, fm_lo = sb("fm_hi", [P, 2, P], F32R), sb("fm_lo", [P, 2, P], F32R)
        fmb = sb("fmb", [P, 1])
        fcb = sb("fcb", [P, D])
        mu_sb = sb("mu_sb", [P, 2, DC])
        id_sb = sb("id_sb", [P, P])
        sign_sb = sb("sign_sb", [P, 1])
        power = sb("power", [P, 2])
        xn = [sb("xn1", [P, 2, D]), sb("xn23", [P, 2, D])]
        stats = [sb("stats1", [P, 2, 6]), sb("stats23", [P, 2, 6])]
        mv = [sb("mv1", [P, 2, 2]), sb("mv23", [P, 2, 2])]
        nmean = [sb("nmean1", [P, 2]), sb("nmean23", [P, 2])]
        veps = [sb("veps1", [P, 2]), sb("veps23", [P, 2])]
        rstd = [sb("rstd1", [P, 2]), sb("rstd23", [P, 2])]
        xt_hi, xt_lo = sb("xt_hi", [P, DC, N], F32R), sb("xt_lo", [P, DC, N], F32R)
        qkt_hi, qkt_lo = sb("qkt_hi", [P, N], F32R), sb("qkt_lo", [P, N], F32R)
        q_st, k_st = sb("q_st", [P, STACK, N], F32R), sb("k_st", [P, STACK, N], F32R)
        v_sb = sb("v_sb", [P, NT, H, VD])
        e_sb = sb("e_sb", [P, E_RING, N])
        nmax = sb("nmax", [P, E_RING])
        esum = sb("esum", [P, 2 * E_RING])
        rsum = sb("rsum", [P, 4, 2])
        ot_hi, ot_lo = sb("ot_hi", [P, 4, N], F32R), sb("ot_lo", [P, 4, N], F32R)
        kf = sb("kf", [P, 4, B, 2, L])
        kblk = sb("kblk", [P, 4, 4, L])
        vblk = sb("vblk", [P, NP, 2 * FE])
        xt2_hi, xt2_lo = sb("xt2_hi", [P, DC, HALF], F32R), sb("xt2_lo", [P, DC, HALF], F32R)
        qf = sb("qf", [P, 4, HALF])
        sx = sb("sx", [P, X_TILES, 512])
        xmax = sb("xmax", [P, 4, 8])
        xsum = sb("xsum", [P, 4, 8])
        xrec = sb("xrec", [P, 4, 8])
        pt_sb = sb("pt_sb", [P, NP, HALF])
        oxt_hi, oxt_lo = sb("oxt_hi", [P, 4, HALF], F32R), sb("oxt_lo", [P, 4, HALF], F32R)
        xt3 = sb("xt3", [P, DC, 1 + N])
        mix_r, mix_k = sb("mix_r", [P, DC, HALF]), sb("mix_k", [P, DC, HALF])
        gate = sb("gate", [P, 2, D])
        kact = sb("kact", [P, DC, HALF])
        wqk_raw = qf[:, :, :].rearrange("p g n -> p (g n)").rearrange("p (c n) -> p c n", c=DC)
        wfc_raw = qf
        wv_raw = pt_sb[:, :, :].rearrange("p g n -> p (g n)").rearrange("p (c n) -> p c n", c=DC)
        wo_raw = v_sb[:, :, H // 2:, :].rearrange("p t h v -> p t (h v)")
        as_raw = "p (t i) n -> p t (i n)"
        ctx_sb = mix_r

        s_bank = [ctx.enter_context(nc.psum_tensor(f"s_bank{i}", [P, 512], F32)) for i in range(S_BANKS)]
        av_bank = [ctx.enter_context(nc.psum_tensor(f"av_bank{i}", [P, 512], F32)) for i in range(AV_BANKS)]
        m_bank = [ctx.enter_context(nc.psum_tensor(f"m_bank{i}", [P, 512], F32)) for i in range(MISC_BANKS)]
        m_bank += s_bank

        stacked = nc.dram_tensor("stacked", (2, 2, 8, 4, KD, N), F32, kind="Internal").ap()

        x_in = [sem(f"x_in{b}") for b in range(B)]
        wqk_in, wv_in, wo_in, wfc_in, id_in = (sem(f"{n}_in") for n in ("wqk", "wv", "wo", "wfc", "id"))
        fm_zero, fm_in, ctx_in, post_in = sem("fm_zero"), sem("fm_in"), sem("ctx_in"), sem("post_in")
        stack_in = [[sem(f"{o}_stack_in{i}") for i in range(STACK)] for o in "qk"]
        stack_out = [[sem(f"{o}_parts_out{c}") for c in range(2)] for o in "qk"]
        res_out = [sem(f"res_out{i}") for i in range(2)]
        filled = [sem(f"filled{i}") for i in range(MISC_BANKS + S_BANKS)]
        emptied = [sem(f"emptied{i}") for i in range(MISC_BANKS + S_BANKS)]
        consts_set, wgt_hi, wgt_lo, fm_ready, fm_cut = (
            sem("consts_set"), sem("wgt_hi"), sem("wgt_lo"), sem("fm_ready"), sem("fm_cut"))
        var_ready = [sem("var_ready1"), sem("var_ready23")]
        rstd_ready = [sem("rstd_ready1"), sem("rstd_ready23")]
        xn_ready = [sem("xn_ready1"), sem("xn_ready23")]
        dve_chain, pool_chain = sem("dve_chain"), sem("pool_chain")
        xt_hi_ready, qk_hi_ready = sem("xt_hi_ready"), sem("qk_hi_ready")
        scores_ready, nmax_ready, exp_ready = sem("scores_ready"), sem("nmax_ready"), sem("exp_ready")
        rsum_ready, v_scaled, av_done = sem("rsum_ready"), sem("v_scaled"), sem("av_done")
        ot_hi_ready, ot_ready = sem("ot_hi_ready"), sem("ot_ready")
        bias_added, kblk_ready = sem("bias_added"), sem("kblk_ready")
        xt2_hi_ready, oxt_hi_ready = sem("xt2_hi_ready"), sem("oxt_hi_ready")
        xexp_ready, xrec_ready, xp_ready = sem("xexp_ready"), sem("xrec_ready"), sem("xp_ready")
        mix_ready, relu_ready, kact_ready, res_ready = (sem("mix_ready"), sem("relu_ready"),
                                                        sem("kact_ready"), sem("res_ready"))

        block = ctx.enter_context(nc.Block())

        def bank(unit):
            return m_bank[uses[unit][0]]

        def wait_filled(eng, unit):
            i, before = uses[unit]
            eng.wait_ge(filled[i], before + 1)

        def wait_emptied(eng, unit):
            i, before = uses[unit]
            eng.wait_ge(emptied[i], before + 1)

        def wait_bank(eng, unit):
            i, before = uses[unit]
            if before:
                eng.wait_ge(emptied[i], before)
            if i >= MISC_BANKS and before == used_before[i - MISC_BANKS]:
                if before or unit[1] == B - 1:
                    eng.wait_ge(exp_ready, TILES)

        def x_at(b, half):
            return b % X_RING * NT + 2 * half

        def lagged(g):
            scale = (g - SCALE_LAG) // 2 if g >= SCALE_LAG and (g - SCALE_LAG) % 2 == 0 else None
            weigh = (g - AV_LAG) // 2 if g >= AV_LAG and (g - AV_LAG) % 2 == 0 else None
            high = (g - OE_LAG) // 8 if g >= OE_LAG and (g - OE_LAG) % 8 == 0 else None
            keep = lambda n, top: n if n is not None and n < top else None
            return keep(scale, TILES // 2), keep(weigh, TILES // 2), keep(high, B * NP)

        @block.sync
        def _(sp):
            xv = x.rearrange("(t p) d -> p t d", p=P)
            sp.dma_start(x_sb[:, 0:NT, :], xv[:, 0:NT, :]).then_inc(x_in[0], 16)
            sp.dma_start(wqk_raw, wqk).then_inc(wqk_in, 16)
            sp.dma_start(id_sb[:], ident).then_inc(id_in, 16)
            sp.dma_start(wv_raw, wv).then_inc(wv_in, 16)

            def load(b, what):
                if what == "o":
                    sp.dma_start(wo_raw, wo.rearrange(as_raw, i=2)).then_inc(wo_in, 16)
                elif what == "fc":
                    sp.wait_ge(wgt_lo, 1)
                    sp.dma_start(wfc_raw[:], wfc).then_inc(wfc_in, 16)
                elif what == "feat":
                    sp.dma_start(ctx_sb[:], ctx_t).then_inc(ctx_in, 16)
                    sp.dma_start(sign_sb[:], sign).then_inc(fm_in, 16)
                    sp.dma_start(fmb[:, :], bass.AP(fm_b.tensor, 0, [[0, 8], [1, KD], [1, 1]])).then_inc(fm_in, 16)
                    sp.wait_ge(fm_zero, 1)
                    for h in range(8):
                        sp.dma_start(fm_sb[h * KD:(h + 1) * KD, h // 4, h % 4, :, :],
                                     bass.AP(fm_t.tensor, 0, [[KD, KD], [0, 2], [1, KD]])).then_inc(fm_in, 16)
                else:
                    for n in range(1, X_RING):
                        sp.dma_start(x_sb[:, n * NT:(n + 1) * NT, :], xv[:, n * NT:(n + 1) * NT, :]).then_inc(x_in[n], 16)
                    sp.dma_start(fcb[:], fc_b.partition_broadcast(P)).then_inc(post_in, 16)
                    sp.dma_start(mu_sb[:], mu).then_inc(post_in, 16)
                    sp.dma_start(wffn_sb[:], wffn).then_inc(post_in, 16)

            def qk_lo(b, c, o):
                wait_emptied(sp, ("qk", b, (c, o)))
                if b:
                    for i in range(STACK):
                        sp.wait_ge(stack_in[o][i], 16 * ((b - 1) * 2 + c + 1))
                for blk in range(4):
                    part = (qkt_hi, qkt_lo)[blk % 2 if o == 0 else blk // 2]
                    sp.dma_start(stacked[o, c, :, blk], part[:, :].bitcast(F32)).then_inc(stack_out[o][c], 16)

            def ld(b, p):
                n = b * NP + p
                for o, st in ((0, q_st), (1, k_st)):
                    sp.wait_ge(stack_out[o][p // 4], 64 * (b + 1))
                    if n >= STACK and o == 0:
                        sp.wait_ge(scores_ready, 8 * (n - STACK + 1))
                    rows = stacked[o, p // 4].rearrange("h k i n -> (h k i) n")
                    at = (p % 4) * P
                    sp.dma_start(st[:, n % STACK, :].bitcast(F32), rows[at:at + P, :]).then_inc(stack_in[o][n % STACK], 16)

            def fv(b, half):
                sp.wait_ge(res_ready, 2 * b + half + 1)
                t, at = b * NT + 2 * half, x_at(b, half)
                sp.dma_start(out.rearrange("(t p) d -> p t d", p=P)[:, t:t + 2, :],
                             x_sb[:, at:at + 2, :]).then_inc(res_out[half], 16)

            def x_load(b):
                if b >= X_RING:
                    for half in range(2):
                        sp.wait_ge(res_out[half], 16 * (b - X_RING + 1))
                    sp.dma_start(x_sb[:, x_at(b, 0):x_at(b, 0) + NT, :], xv[:, b * NT:(b + 1) * NT, :])\
                      .then_inc(x_in[b], 16)

            parts = {"load": load, "x_load": x_load, "qk_lo": qk_lo, "ld": ld, "fv": fv}
            for g, stages in steps:
                for name, b, args in stages:
                    if name in parts:
                        parts[name](b, *args)
            for half in range(2):
                sp.wait_ge(res_out[half], 16 * B)


        @block.tensor
        def _(pe):
            def matmul3(dst, a_hi, a_lo, b_hi, b_lo, first, last):
                pe.matmul(dst, a_hi, b_hi, start=first, stop=False)
                pe.matmul(dst, a_lo, b_hi, start=False, stop=False)
                return pe.matmul(dst, a_hi, b_lo, start=False, stop=last)

            def scores(g):
                n, j = g // 8, g % 8
                m, par = j // 2, j % 2
                if j == 0:
                    pe.wait_ge(stack_in[0][n % STACK], 16 * (n // STACK + 1))
                    pe.wait_ge(stack_in[1][n % STACK], 16 * (n // STACK + 1))
                if g >= S_BANKS:
                    pe.wait_ge(exp_ready, g - S_BANKS + 1)
                elif used_before[g]:
                    pe.wait_ge(emptied[MISC_BANKS + g], used_before[g])
                rows = slice(64 * par, 64 * par + 64)
                pe.matmul(s_bank[g % S_BANKS][:, :], k_st[rows, n % STACK, m * P:(m + 1) * P],
                          q_st[rows, n % STACK, :], start=True, stop=True).then_inc(scores_ready, 1)

            def weigh(n):
                m, p = n % NT, (n // NT) % NP
                if m == 0 and n // NT >= AV_BANKS:
                    pe.wait_ge(ot_ready, n // NT - AV_BANKS + 1)
                pe.wait_ge(v_scaled, n + 1)
                for par in range(2):
                    mm = pe.matmul(av_bank[n // NT % AV_BANKS][64 * par:64 * par + 64, :], v_sb[:, m, 2 * p + par, :],
                                   e_sb[:, (2 * n + par) % E_RING, :], start=(m == 0), stop=(m == NT - 1))
                mm.then_inc(av_done, 1)

            def transposed(k):
                def t(b, half):
                    unit = (f"t{k}", b, (half,))
                    wait_bank(pe, unit)
                    i = k > 1
                    count = 2 * b + half if k == 1 else 4 * b + 2 * (k - 2) + half
                    pe.wait_ge(xn_ready[i], count + 1)
                    if unit == ("t1", 0, (0,)):
                        pe.wait_ge(id_in, 16)
                    for c in range(DC):
                        for t2 in range(2):
                            mm = pe.transpose(bank(unit)[:, c * HALF + t2 * P:c * HALF + (t2 + 1) * P],
                                              xn[i][:, t2, c * P:(c + 1) * P], id_sb[:, :])
                    mm.then_inc(filled[uses[unit][0]], 1)
                return t

            def qk(b, c, o):
                unit = ("qk", b, (c, o))
                wait_bank(pe, unit)
                for half in range(2):
                    wait_emptied(pe, ("t1", b, (half,)))
                if b == 0:
                    pe.wait_ge(wgt_lo, 1)
                cols = slice(o * D + c * P, o * D + (c + 1) * P)
                for d in range(DC):
                    mm = matmul3(bank(unit)[:, :], wqk_hi[:, d, cols], wqk_lo[:, d, cols],
                                 xt_hi[:, d, :], xt_lo[:, d, :], d == 0, d == DC - 1)
                mm.then_inc(filled[uses[unit][0]], 1)

            def v(b, hh, m):
                unit = ("v", b, (hh, m))
                wait_bank(pe, unit)
                wait_emptied(pe, ("t1", b, (m // 2,)))
                if b == 0:
                    pe.wait_ge(wgt_lo, 2)
                for d in range(DC):
                    mm = matmul3(bank(unit)[:, :], xt_hi[:, d, m * P:(m + 1) * P], xt_lo[:, d, m * P:(m + 1) * P],
                                 wv_hi[:, d, hh * 512:(hh + 1) * 512], wv_lo[:, d, hh * 512:(hh + 1) * 512],
                                 d == 0, d == DC - 1)
                mm.then_inc(filled[uses[unit][0]], 1)

            def op(b, hh, tt):
                unit = ("op", b, (hh, tt))
                wait_bank(pe, unit)
                pe.wait_ge(ot_ready, b * NP + 4 * hh + 4)
                if b == 0 and hh == 0:
                    pe.wait_ge(wgt_lo, 4)
                for t2 in range(2):
                    at = (2 * tt + t2) * P
                    for p in range(4):
                        mm = matmul3(bank(unit)[:, t2 * D:(t2 + 1) * D], ot_hi[:, p, at:at + P], ot_lo[:, p, at:at + P],
                                     wo_hi[:, 4 * hh + p, :], wo_lo[:, 4 * hh + p, :], p == 0, p == 3)
                mm.then_inc(filled[uses[unit][0]], 1)

            def kf_(b, gg):
                unit = ("kf", b, (gg,))
                wait_bank(pe, unit)
                pe.wait_ge(fm_ready, 1)
                pe.wait_ge(ctx_in, 16)
                for i in range(2):
                    mm = pe.matmul(bank(unit)[:, i * HALF:(i + 1) * HALF],
                                   fm_sb[:, i].rearrange("p h s e -> p (h s e)"), ctx_sb[:, gg, :],
                                   start=True, stop=True)
                mm.then_inc(filled[uses[unit][0]], 1)

            def kv(b):
                unit = ("kv", b, ())
                wait_bank(pe, unit)
                for gg in range(2):
                    wait_emptied(pe, ("kf", 0, (gg,)))
                for i in range(4):
                    mm = pe.transpose(bank(unit)[:, i * P:(i + 1) * P], kf[:, i, b].rearrange("p r l -> p (r l)"),
                                      id_sb[:, :])
                mm.then_inc(filled[uses[unit][0]], 1)

            def z(b, half, gg):
                unit = ("z", b, (half, gg))
                wait_bank(pe, unit)
                wait_emptied(pe, ("t2", b, (half,)))
                if b == 0:
                    pe.wait_ge(fm_cut, 2)
                for i in range(2):
                    mm = matmul3(bank(unit)[:, i * HALF:(i + 1) * HALF], fm_hi[:, i], fm_lo[:, i],
                                 xt2_hi[:, gg, :], xt2_lo[:, gg, :], True, True)
                mm.then_inc(filled[uses[unit][0]], 1)

            def xs(b, t, gg):
                unit = ("xs", b, (t, gg))
                wait_bank(pe, unit)
                wait_emptied(pe, ("z", b, (t // 2, gg)))
                if t == 0:
                    pe.wait_ge(kblk_ready, b + 1)
                for i in range(2):
                    mm = pe.matmul(bank(unit)[:, i * HALF:(i + 1) * HALF],
                                   qf[:, 2 * gg + i, (t % 2) * P:(t % 2 + 1) * P],
                                   kblk[:, 2 * gg + i].rearrange("p h l -> p (h l)"), start=True, stop=True)
                mm.then_inc(filled[uses[unit][0]], 1)

            def pt(b, t, gg):
                unit = ("pt", b, (t, gg))
                wait_bank(pe, unit)
                n = 8 * b + 2 * t + gg
                pe.wait_ge(xp_ready, n + 1)
                for i in range(4):
                    mm = pe.transpose(bank(unit)[:, i * P:(i + 1) * P], sx[:, n % X_TILES, i * P:(i + 1) * P], id_sb[:, :])
                mm.then_inc(filled[uses[unit][0]], 1)

            def pv(b, half, gg):
                unit = ("pv", b, (half, gg))
                wait_bank(pe, unit)
                for t in (2 * half, 2 * half + 1):
                    wait_emptied(pe, ("pt", b, (t, gg)))
                wait_emptied(pe, ("kv", b, ()))
                for i in range(2):
                    for q in range(2):
                        pair = 4 * gg + 2 * i + q
                        mm = pe.matmul(bank(unit)[64 * q:64 * q + 64, i * HALF:(i + 1) * HALF], vblk[:, pair, :],
                                       pt_sb[:, pair, :], start=True, stop=True)
                mm.then_inc(filled[uses[unit][0]], 1)

            def fc(b, half):
                unit = ("fc", b, (half,))
                wait_bank(pe, unit)
                for gg in range(2):
                    wait_emptied(pe, ("pv", b, (half, gg)))
                if b == 0:
                    pe.wait_ge(post_in, 48)
                for t2 in range(2):
                    for i in range(4):
                        at = slice(t2 * P, (t2 + 1) * P)
                        mm = matmul3(bank(unit)[:, t2 * D:(t2 + 1) * D], oxt_hi[:, i, at], oxt_lo[:, i, at],
                                     wfc_hi[:, i, :], wfc_lo[:, i, :], i == 0, i == 3)
                mm.then_inc(filled[uses[unit][0]], 1)

            def fr(b, half):
                unit = ("fr", b, (half,))
                wait_bank(pe, unit)
                pe.wait_ge(mix_ready, 2 * b + half + 1)
                for t2 in range(2):
                    for c in range(DC):
                        mm = pe.matmul(bank(unit)[:, t2 * D:(t2 + 1) * D], mix_r[:, c, t2 * P:(t2 + 1) * P],
                                       wffn_sb[:, 0, c, :], start=(c == 0), stop=(c == DC - 1))
                mm.then_inc(filled[uses[unit][0]], 1)

            def fk(b, half):
                unit = ("fk", b, (half,))
                wait_bank(pe, unit)
                pe.wait_ge(mix_ready, 2 * b + half + 1)
                for mc in range(DC):
                    for c in range(DC):
                        mm = pe.matmul(bank(unit)[:, mc * HALF:(mc + 1) * HALF],
                                       wffn_sb[:, 1, c, mc * P:(mc + 1) * P], mix_k[:, c, :],
                                       start=(c == 0), stop=(c == DC - 1))
                mm.then_inc(filled[uses[unit][0]], 1)

            def fv(b, half):
                unit = ("fv", b, (half,))
                wait_bank(pe, unit)
                pe.wait_ge(kact_ready, 2 * b + half + 1)
                for t2 in range(2):
                    for c in range(DC):
                        mm = pe.matmul(bank(unit)[:, t2 * D:(t2 + 1) * D], kact[:, c, t2 * P:(t2 + 1) * P],
                                       wffn_sb[:, 2, c, :], start=(c == 0), stop=(c == DC - 1))
                mm.then_inc(filled[uses[unit][0]], 1)

            parts = {"t1": transposed(1), "t2": transposed(2), "t3": transposed(3), "qk": qk, "v": v, "op": op,
                     "kf": kf_, "kv": kv, "z": z, "xs": xs, "pt": pt, "pv": pv, "fc": fc, "fr": fr, "fk": fk, "fv": fv}
            for g, stages in steps:
                if 0 <= g < TILES:
                    scores(g)
                _, n, _ = lagged(g)
                if n is not None:
                    weigh(n)
                for name, b, args in stages:
                    if name in parts:
                        parts[name](b, *args)

        @block.scalar
        def _(act):
            def exponentials(g):
                act.wait_ge(nmax_ready, g + 1)
                if g >= E_RING:
                    act.wait_ge(av_done, (g - E_RING) // 2 + 1)
                act.activation(e_sb[:, g % E_RING, :], s_bank[g % S_BANKS][:, :], ACT.Exp,
                               bias=nmax[:, g % E_RING:g % E_RING + 1],
                               accum_out=esum[:, g % (2 * E_RING):g % (2 * E_RING) + 1]).then_inc(exp_ready, 1)

            def ot_high(n):
                act.wait_ge(av_done, NT * (n + 1))
                if n >= 4:
                    last = (n // 4 - 1)
                    wait_filled(act, ("op", last // 2, (last % 2, 1)))
                act.activation(ot_hi[:, n % 4, :], av_bank[n % AV_BANKS][:, :], ACT.Copy).then_inc(ot_hi_ready, 1)

            def cut(b, which):
                if which == "qk":
                    act.wait_ge(wqk_in, 16)
                    act.activation(wqk_hi[:, :, 0:D], wqk_raw[:, :, 0:D], ACT.Copy, scale=KD ** -0.5)
                    act.activation(wqk_hi[:, :, D:], wqk_raw[:, :, D:], ACT.Copy).then_inc(wgt_hi, 1)
                elif which == "v":
                    act.wait_ge(wv_in, 16)
                    act.activation(wv_hi[:, :, :], wv_raw, ACT.Copy).then_inc(wgt_hi, 1)
                elif which == "fc":
                    act.wait_ge(wfc_in, 16)
                    act.activation(wfc_hi[:, :, :], wfc_raw[:, :, :], ACT.Copy).then_inc(wgt_hi, 1)
                else:
                    act.wait_ge(wo_in, 16)
                    act.activation(wo_hi[:, :, :].rearrange(as_raw, i=2), wo_raw, ACT.Copy).then_inc(wgt_hi, 1)

            def feat(b):
                act.wait_ge(fm_ready, 1)
                act.activation(fm_hi[:, :, :], fm_sb[:, :, :, :, :].rearrange("p g h s e -> p g (h s e)"), ACT.Copy)\
                   .then_inc(fm_cut, 1)

            def t1(b, half):
                unit = ("t1", b, (half,))
                wait_filled(act, unit)
                if b:
                    wait_filled(act, ("v", b - 1, (1, NT - 1)))
                    wait_filled(act, ("qk", b - 1, (1, 1)))
                act.activation(xt_hi[:, :, half * HALF:(half + 1) * HALF],
                               bank(unit)[:, :].rearrange("p (c n) -> p c n", c=DC), ACT.Copy).then_inc(xt_hi_ready, 1)

            def qk(b, c, o):
                unit = ("qk", b, (c, o))
                wait_filled(act, unit)
                if (b, c, o) != (0, 0, 0):
                    n = 4 * b + 2 * c + o - 1
                    act.wait_ge(stack_out[n % 2][n // 2 % 2], 64 * (n // 4 + 1))
                act.activation(qkt_hi[:, :], bank(unit)[:, :], ACT.Copy).then_inc(qk_hi_ready, 1)

            def v(b, hh, m):
                if m % 2 == 0:
                    unit = ("v", b, (hh, m))
                    wait_filled(act, unit)
                    if b == 0 and hh:
                        act.wait_ge(wgt_lo, 4)
                    if b:
                        act.wait_ge(av_done, NT * ((b - 1) * NP + 4 * hh + 4))
                    act.activation(v_sb[:, m, 8 * hh:8 * hh + 8, :],
                                   bank(unit)[:, :].rearrange("p (h v) -> p h v", h=8), ACT.Copy)\
                       .then_inc(emptied[uses[unit][0]], 1)

            def kf_(b, gg):
                unit = ("kf", b, (gg,))
                wait_filled(act, unit)
                for twice in range(2):
                    for i in range(2):
                        ins = act.activation(kf[:, 2 * gg + i, :, twice, :],
                                             bank(unit)[:, i * HALF:(i + 1) * HALF].rearrange("p (b l) -> p b l", b=B),
                                             ACT.Exp, bias=fmb[:, 0:1])
                ins.then_inc(emptied[uses[unit][0]], 1)

            def t2(b, half):
                unit = ("t2", b, (half,))
                wait_filled(act, unit)
                if (b, half) != (0, 0):
                    pb, ph = (b, 0) if half else (b - 1, 1)
                    wait_filled(act, ("z", pb, (ph, 1)))
                act.activation(xt2_hi[:, :, :], bank(unit)[:, :].rearrange("p (c n) -> p c n", c=DC), ACT.Copy)\
                   .then_inc(xt2_hi_ready, 1)

            def z(b, half, gg):
                unit = ("z", b, (half, gg))
                wait_filled(act, unit)
                if (b, half) != (0, 0):
                    pb, ph = (b, 0) if half else (b - 1, 1)
                    wait_filled(act, ("xs", pb, (2 * ph + 1, gg)))
                act.activation(qf[:, 2 * gg:2 * gg + 2, :], bank(unit)[:, :].rearrange("p (g n) -> p g n", g=2),
                               ACT.Exp, bias=fmb[:, 0:1]).then_inc(emptied[uses[unit][0]], 1)

            def xs(b, t, gg):
                n = 8 * b + 2 * t + gg
                wait_emptied(act, ("xs", b, (t, gg)))
                act.activation(sx[:, n % X_TILES, :], sx[:, n % X_TILES, :], ACT.Exp).then_inc(xexp_ready, 1)

            def pt(b, t, gg):
                unit = ("pt", b, (t, gg))
                wait_filled(act, unit)
                if (b, t) >= (0, 2):
                    pb, ph = (b, 0) if t >= 2 else (b - 1, 1)
                    wait_filled(act, ("pv", pb, (ph, gg)))
                act.activation(pt_sb[:, 4 * gg:4 * gg + 4, (t % 2) * P:(t % 2 + 1) * P],
                               bank(unit)[:, :].rearrange("p (i n) -> p i n", i=4), ACT.Copy)\
                   .then_inc(emptied[uses[unit][0]], 1)

            def pv(b, half, gg):
                unit = ("pv", b, (half, gg))
                wait_filled(act, unit)
                if (b, half) != (0, 0):
                    pb, ph = (b, 0) if half else (b - 1, 1)
                    wait_filled(act, ("fc", pb, (ph,)))
                act.activation(oxt_hi[:, 2 * gg:2 * gg + 2, :], bank(unit)[:, :].rearrange("p (i n) -> p i n", i=2),
                               ACT.Copy).then_inc(oxt_hi_ready, 1)

            def t3(b, half):
                unit = ("t3", b, (half,))
                wait_filled(act, unit)
                if b and half == 0:
                    act.wait_ge(mix_ready, 2 * b)
                act.activation(xt3[:, :, 1 + half * HALF:1 + (half + 1) * HALF],
                               bank(unit)[:, :].rearrange("p (c n) -> p c n", c=DC), ACT.Copy)\
                   .then_inc(emptied[uses[unit][0]], 1)

            def fr(b, half):
                unit = ("fr", b, (half,))
                wait_filled(act, unit)
                n = 2 * b + half
                if n:
                    act.wait_ge(res_ready, n)
                act.activation(gate[:, :, :], bank(unit)[:, :].rearrange("p (t d) -> p t d", t=2), ACT.Tanh,
                               scale=0.5).then_inc(emptied[uses[unit][0]], 1)

            def fk(b, half):
                unit = ("fk", b, (half,))
                wait_filled(act, unit)
                if (b, half) != (0, 0):
                    pb, ph = (b, 0) if half else (b - 1, 1)
                    wait_filled(act, ("fv", pb, (ph,)))
                act.activation(kact[:, :, :], bank(unit)[:, :].rearrange("p (c n) -> p c n", c=DC), ACT.Relu)\
                   .then_inc(emptied[uses[unit][0]], 1)

            parts = {"cut": cut, "feat": feat, "t1": t1, "qk": qk, "v": v, "kf": kf_, "t2": t2, "z": z, "xs": xs, "pt": pt,
                     "pv": pv, "t3": t3, "fr": fr, "fk": fk}
            for g, stages in steps:
                _, _, n = lagged(g)
                if n is not None:
                    ot_high(n)
                if 0 <= g < TILES:
                    exponentials(g)
                for name, b, args in stages:
                    if name in parts:
                        parts[name](b, *args)

        @block.vector
        def _(dve):
            chained = [0]

            def link(ins):
                chained[0] += 1
                ins.then_inc(dve_chain, 1)
                dve.wait_ge(dve_chain, chained[0])

            dve.memset(vblk[:, :, :], 0.0).then_inc(consts_set, 1)

            def maxima(g):
                dve.wait_ge(scores_ready, g + 1)
                dve.tensor_reduce(nmax[:, g % E_RING:g % E_RING + 1], s_bank[g % S_BANKS][:, :], AX_X, ALU.max,
                                  negate=True).then_inc(nmax_ready, 1)

            def row_sums(n):
                dve.wait_ge(exp_ready, 2 * n + 2)
                at = (2 * n) % (2 * E_RING)
                if n >= 4:
                    dve.wait_ge(v_scaled, n - 3)
                dve.reciprocal(rsum[:, n % 4, :], esum[:, at:at + 2]).then_inc(rsum_ready, 1)

            def ot_low(n):
                dve.wait_ge(ot_hi_ready, n + 1)
                dve.tensor_tensor(ot_lo[:, n % 4, :], av_bank[n % AV_BANKS][:, :], ot_hi[:, n % 4, :].bitcast(F32), ALU.subtract)\
                   .then_inc(ot_ready, 1)

            def cut(b, which):
                if which == "qk":
                    dve.wait_ge(wgt_hi, 1)
                    dve.scalar_tensor_tensor(out=wqk_lo[:, :, 0:D], in0=wqk_raw[:, :, 0:D], scalar=KD ** -0.5,
                                             in1=wqk_hi[:, :, 0:D].bitcast(F32), op0=ALU.mult, op1=ALU.subtract)
                    dve.tensor_tensor(wqk_lo[:, :, D:], wqk_raw[:, :, D:], wqk_hi[:, :, D:].bitcast(F32),
                                      ALU.subtract).then_inc(wgt_lo, 1)
                elif which == "v":
                    dve.wait_ge(wgt_hi, 2)
                    dve.tensor_tensor(wv_lo[:, :, :], wv_raw, wv_hi[:, :, :].bitcast(F32), ALU.subtract)\
                       .then_inc(wgt_lo, 1)
                elif which == "fc":
                    dve.wait_ge(wgt_hi, 3)
                    dve.tensor_tensor(wfc_lo[:, :, :], wfc_raw[:, :, :], wfc_hi[:, :, :].bitcast(F32), ALU.subtract)\
                       .then_inc(wgt_lo, 1)
                else:
                    dve.wait_ge(wgt_hi, 4)
                    dve.tensor_tensor(wo_lo[:, :, :].rearrange(as_raw, i=2), wo_raw,
                                      wo_hi[:, :, :].bitcast(F32).rearrange(as_raw, i=2), ALU.subtract)\
                       .then_inc(wgt_lo, 1)

            def norm_stats(k):
                def ln(b, half):
                    i = k > 1
                    count = 2 * b + half if k == 1 else 4 * b + 2 * (k - 2) + half
                    if k == 1:
                        dve.wait_ge(x_in[b], 16)
                    elif k == 2:
                        wait_emptied(dve, ("op", b, (1, half)))
                    else:
                        wait_emptied(dve, ("fc", b, (half,)))
                    if count:
                        dve.wait_ge(xn_ready[i], count)
                    for t2 in range(2):
                        ins = dve.bn_stats(stats[i][:, t2, :], x_sb[:, x_at(b, half) + t2, :])
                    link(ins)
                    for t2 in range(2):
                        ins = dve.bn_aggr(mv[i][:, t2, :], stats[i][:, t2, :])
                    link(ins)
                    dve.tensor_scalar(nmean[i][:, :], mv[i][:, :, 0], -1.0, None, ALU.mult)
                    dve.tensor_scalar(veps[i][:, :], mv[i][:, :, 1], EPS, None, ALU.add).then_inc(var_ready[i], 1)
                return ln

            def t1_lo(b, half):
                unit = ("t1", b, (half,))
                dve.wait_ge(xt_hi_ready, 2 * b + half + 1)
                at = slice(half * HALF, (half + 1) * HALF)
                dve.tensor_tensor(xt_lo[:, :, at], bank(unit)[:, :].rearrange("p (c n) -> p c n", c=DC),
                                  xt_hi[:, :, at].bitcast(F32), ALU.subtract).then_inc(emptied[uses[unit][0]], 1)

            def qk_lo(b, c, o):
                unit = ("qk", b, (c, o))
                dve.wait_ge(qk_hi_ready, 4 * b + 2 * c + o + 1)
                dve.tensor_tensor(qkt_lo[:, :], bank(unit)[:, :], qkt_hi[:, :].bitcast(F32), ALU.subtract)\
                   .then_inc(emptied[uses[unit][0]], 1)

            def v(b, hh, m):
                if m % 2:
                    unit = ("v", b, (hh, m))
                    wait_filled(dve, unit)
                    if b == 0 and hh:
                        dve.wait_ge(wgt_lo, 4)
                    if b:
                        dve.wait_ge(av_done, NT * ((b - 1) * NP + 4 * hh + 4))
                    dve.tensor_copy(v_sb[:, m, 8 * hh:8 * hh + 8, :],
                                    bank(unit)[:, :].rearrange("p (h v) -> p h v", h=8))\
                       .then_inc(emptied[uses[unit][0]], 1)

            def op(b, hh, tt):
                unit = ("op", b, (hh, tt))
                wait_filled(dve, unit)
                at = x_at(b, tt)
                if hh:
                    wait_emptied(dve, ("op", b, (0, tt)))
                dve.tensor_tensor(x_sb[:, at:at + 2, :], bank(unit)[:, :].rearrange("p (t d) -> p t d", t=2),
                                  x_sb[:, at:at + 2, :], ALU.add).then_inc(emptied[uses[unit][0]], 1)

            def feat(b):
                dve.wait_ge(fm_in, 16 * 10)
                dve.tensor_scalar(fm_sb[:, :, :, 1, :].rearrange("p g h e -> p (g h) e"),
                                  fm_sb[:, :, :, 1, :].rearrange("p g h e -> p (g h) e"), -1.0, None, ALU.mult)
                dve.tensor_tensor(fmb[:, :], fmb[:, :], sign_sb[:, :], ALU.mult).then_inc(fm_ready, 1)
                dve.wait_ge(fm_cut, 1)
                dve.tensor_tensor(fm_lo[:, :, :], fm_sb[:, :, :, :, :].rearrange("p g h s e -> p g (h s e)"),
                                  fm_hi[:, :, :].bitcast(F32), ALU.subtract).then_inc(fm_cut, 1)

            def t2_lo(b, half):
                unit = ("t2", b, (half,))
                dve.wait_ge(xt2_hi_ready, 2 * b + half + 1)
                dve.tensor_tensor(xt2_lo[:, :, :], bank(unit)[:, :].rearrange("p (c n) -> p c n", c=DC),
                                  xt2_hi[:, :, :].bitcast(F32), ALU.subtract).then_inc(emptied[uses[unit][0]], 1)

            def pv_lo(b, half, gg):
                unit = ("pv", b, (half, gg))
                dve.wait_ge(oxt_hi_ready, 4 * b + 2 * half + gg + 1)
                at = slice(2 * gg, 2 * gg + 2)
                dve.tensor_tensor(oxt_lo[:, at, :], bank(unit)[:, :].rearrange("p (i n) -> p i n", i=2),
                                  oxt_hi[:, at, :].bitcast(F32), ALU.subtract).then_inc(emptied[uses[unit][0]], 1)

            def kv(b):
                unit = ("kv", b, ())
                wait_filled(dve, unit)
                if b:
                    wait_filled(dve, ("xs", b - 1, (NT - 1, 0)))
                    wait_filled(dve, ("xs", b - 1, (NT - 1, 1)))
                else:
                    dve.wait_ge(consts_set, 2)
                for h in range(4):
                    ins = dve.tensor_scalar(kblk[32 * h:32 * h + 32, :, h, :], kf[32 * h:32 * h + 32, :, b, 0, :],
                                            D ** -0.5, None, ALU.mult)
                ins.then_inc(kblk_ready, 1)
                if b:
                    wait_filled(dve, ("pv", b - 1, (1, 1)))
                v4 = bank(unit)[:, :].rearrange("p (r q s) -> p r q s", q=2, s=FE)
                for q in range(2):
                    ins = dve.tensor_copy(vblk[64 * q:64 * q + 64, :, q * FE:(q + 1) * FE],
                                          v4[64 * q:64 * q + 64, :, q, :])
                ins.then_inc(emptied[uses[unit][0]], 1)

            def xs(b, t, gg):
                unit = ("xs", b, (t, gg))
                wait_filled(dve, unit)
                n = 8 * b + 2 * t + gg
                src = bank(unit)[:, :].rearrange("p (h l) -> p h l", h=8)
                link(dve.tensor_reduce(xmax[:, n % 4, :], src, AX_X, ALU.max, negate=True))
                if n >= X_TILES:
                    pb, r = (n - X_TILES) // 8, (n - X_TILES) % 8
                    wait_filled(dve, ("pt", pb, (r // 2, r % 2)))
                dve.tensor_tensor(sx[:, n % X_TILES, :].rearrange("p (h l) -> p h l", h=8), src,
                                  xmax[:, n % 4, :].unsqueeze(2).broadcast_to([P, 8, L]), ALU.add)\
                   .then_inc(emptied[uses[unit][0]], 1)

            def xn_(b, t, gg):
                n = 8 * b + 2 * t + gg
                dve.wait_ge(xexp_ready, n + 1)
                link(dve.tensor_reduce(xsum[:, n % 4, :], sx[:, n % X_TILES, :].rearrange("p (h l) -> p h l", h=8),
                                       AX_X, ALU.add))
                if n >= 4:
                    dve.wait_ge(xp_ready, n - 3)
                dve.reciprocal(xrec[:, n % 4, :], xsum[:, n % 4, :]).then_inc(xrec_ready, 1)

            def fc(b, half):
                unit = ("fc", b, (half,))
                wait_filled(dve, unit)
                dve.wait_ge(bias_added, 2 * b + half + 1)
                at = x_at(b, half)
                dve.tensor_tensor(x_sb[:, at:at + 2, :], bank(unit)[:, :].rearrange("p (t d) -> p t d", t=2),
                                  x_sb[:, at:at + 2, :], ALU.add).then_inc(emptied[uses[unit][0]], 1)

            def mix(b, half):
                wait_emptied(dve, ("t3", b, (half,)))
                n = 2 * b + half
                if n == 0:
                    dve.wait_ge(post_in, 48)
                if n:
                    pb, ph = (b, 0) if half else (b - 1, 1)
                    wait_filled(dve, ("fr", pb, (ph,)))
                    wait_filled(dve, ("fk", pb, (ph,)))
                cur = xt3[:, :, 1 + half * HALF:1 + (half + 1) * HALF]
                prev = xt3[:, :, half * HALF:(half + 1) * HALF]
                link(dve.tensor_tensor(mix_k[:, :, :], cur, prev, ALU.subtract))
                for c in range(DC):
                    ins = dve.scalar_tensor_tensor(out=mix_r[:, c, :], in0=mix_k[:, c, :], scalar=mu_sb[:, 0, c:c + 1],
                                                   in1=prev[:, c, :], op0=ALU.mult, op1=ALU.add)
                link(ins)
                for c in range(DC):
                    ins = dve.scalar_tensor_tensor(out=mix_k[:, c, :], in0=mix_k[:, c, :], scalar=mu_sb[:, 1, c:c + 1],
                                                   in1=prev[:, c, :], op0=ALU.mult, op1=ALU.add)
                ins.then_inc(mix_ready, 1)

            def fv(b, half):
                unit = ("fv", b, (half,))
                wait_filled(dve, unit)
                wait_emptied(dve, ("fr", b, (half,)))
                at = x_at(b, half)
                dve.scalar_tensor_tensor(out=gate[:, :, :], in0=gate[:, :, :], scalar=1.0,
                                         in1=bank(unit)[:, :].rearrange("p (t d) -> p t d", t=2),
                                         op0=ALU.add, op1=ALU.mult).then_inc(emptied[uses[unit][0]], 1)
                wait_emptied(dve, unit)
                dve.scalar_tensor_tensor(out=x_sb[:, at:at + 2, :], in0=gate[:, :, :], scalar=0.5,
                                         in1=x_sb[:, at:at + 2, :], op0=ALU.mult, op1=ALU.add).then_inc(res_ready, 1)

            parts = {"cut": cut, "ln1": norm_stats(1), "ln2": norm_stats(2), "ln3": norm_stats(3), "t1_lo": t1_lo,
                     "t2_lo": t2_lo, "pv_lo": pv_lo,
                     "qk_lo": qk_lo, "v": v, "op": op, "feat": feat, "kv": kv, "xs": xs, "xn": xn_, "fc": fc,
                     "mix": mix, "fv": fv}
            for g, stages in steps:
                n, _, pair = lagged(g)
                if pair is not None:
                    ot_low(pair)
                if 0 <= g < TILES:
                    maxima(g)
                if n is not None:
                    row_sums(n)
                for name, b, args in stages:
                    if name in parts:
                        parts[name](b, *args)

        @block.gpsimd
        def _(pool):
            pool.memset(fm_sb[:, :, :, :, :], 0.0).then_inc(fm_zero, 1)
            pool.memset(power[:, :], -0.5).then_inc(pool_chain, 1)
            pool.memset(kblk[:, :, :, :], 0.0).then_inc(pool_chain, 1)
            pool.memset(xt3[:, :, 0:1], 0.0).then_inc(consts_set, 1)
            pool.wait_ge(pool_chain, 2)

            def scale_values(n):
                m, p = n % NT, (n // NT) % NP
                pool.wait_ge(rsum_ready, n + 1)
                if p % 4 == 0:
                    wait_emptied(pool, ("v", n // (NT * NP), (p // 4, m)))
                pool.tensor_tensor(v_sb[:, m, 2 * p:2 * p + 2, :], v_sb[:, m, 2 * p:2 * p + 2, :],
                                   rsum[:, n % 4, :].unsqueeze(2).broadcast_to([P, 2, VD]), ALU.mult)\
                    .then_inc(v_scaled, 1)

            def norm_apply(k):
                def ln(b, half):
                    i = k > 1
                    count = 2 * b + half if k == 1 else 4 * b + 2 * (k - 2) + half
                    pool.wait_ge(var_ready[i], count + 1)
                    pool.tensor_tensor(rstd[i][:, :], veps[i][:, :], power[:, :], ALU.pow).then_inc(rstd_ready[i], 1)
                    pool.wait_ge(rstd_ready[i], count + 1)
                    if k == 1 and count:
                        pb, ph = (b, 0) if half else (b - 1, 1)
                        wait_filled(pool, ("t1", pb, (ph,)))
                    elif k > 1 and count:
                        pk, pb, ph = (k, b, 0) if half else (2, b, 1) if k == 3 else (3, b - 1, 1)
                        wait_filled(pool, (f"t{pk}", pb, (ph,)))
                    for t2 in range(2):
                        ins = pool.tensor_scalar(xn[i][:, t2, :], x_sb[:, x_at(b, half) + t2, :],
                                                 nmean[i][:, t2:t2 + 1], rstd[i][:, t2:t2 + 1], ALU.add, ALU.mult)
                    ins.then_inc(xn_ready[i], 1)
                    if k == 2:
                        pool.wait_ge(xn_ready[i], count + 1)
                        if count == 0:
                            pool.wait_ge(post_in, 48)
                        at = x_at(b, half)
                        pool.tensor_tensor(x_sb[:, at:at + 2, :], x_sb[:, at:at + 2, :],
                                           fcb[:, :].unsqueeze(1).broadcast_to([P, 2, D]), ALU.add)\
                            .then_inc(bias_added, 1)
                return ln

            def xn_(b, t, gg):
                n = 8 * b + 2 * t + gg
                pool.wait_ge(xrec_ready, n + 1)
                sx3 = sx[:, n % X_TILES, :].rearrange("p (h l) -> p h l", h=8)
                pool.tensor_tensor(sx3, sx3, xrec[:, n % 4, :].unsqueeze(2).broadcast_to([P, 8, L]), ALU.mult)\
                    .then_inc(xp_ready, 1)

            def fk(b, half):
                wait_emptied(pool, ("fk", b, (half,)))
                pool.tensor_tensor(kact[:, :, :], kact[:, :, :], kact[:, :, :], ALU.mult).then_inc(kact_ready, 1)

            parts = {"ln1": norm_apply(1), "ln2": norm_apply(2), "ln3": norm_apply(3), "xn": xn_, "fk": fk}
            for g, stages in steps:
                n, _, _ = lagged(g)
                if n is not None:
                    scale_values(n)
                for name, b, args in stages:
                    if name in parts:
                        parts[name](b, *args)


def kernel(x, ctx_1024, L0_attn_query_proj, L0_attn_key_proj, L0_attn_value_proj, L0_attn_output_proj,
           L0_xattn_fm_w, L0_xattn_fm_b, L0_xattn_fc_w, L0_xattn_fc_b, L0_ffn_W_r, L0_ffn_W_k, L0_ffn_W_v,
           L0_ffn_mu_r, L0_ffn_mu_k):
    import numpy as np
    import concourse.bacc as bacc
    from concourse.bass_utils import run_bass_kernel_spmd

    def rows(a, c):
        return np.ascontiguousarray(np.reshape(a, (c, P, -1)).transpose(1, 0, 2))

    wq = np.asarray(L0_attn_query_proj).transpose(2, 1, 0).reshape(D, H * KD)
    wk = np.asarray(L0_attn_key_proj).transpose(2, 0, 1).reshape(D, H * KD)
    arrays = {
        "x": np.asarray(x).reshape(B * N, D),
        "ctx_t": rows(np.asarray(ctx_1024).transpose(2, 0, 1).reshape(D, B * L), DC),
        "wqk": rows(np.concatenate([wq, wk], axis=1), DC),
        "wv": rows(np.asarray(L0_attn_value_proj).transpose(2, 0, 1).reshape(D, H * VD), DC),
        "wo": rows(np.asarray(L0_attn_output_proj).transpose(1, 2, 0).reshape(H * VD, D), NP),
        "fm_t": np.ascontiguousarray(np.asarray(L0_xattn_fm_w).T),
        "fm_b": np.asarray(L0_xattn_fm_b).reshape(KD, 1),
        "wfc": rows(np.asarray(L0_xattn_fc_w).T, 4),
        "fc_b": np.asarray(L0_xattn_fc_b),
        "wffn": np.ascontiguousarray(np.stack([rows(np.asarray(w).T, DC) for w in (L0_ffn_W_r, L0_ffn_W_k, L0_ffn_W_v)], axis=1)),
        "mu": np.ascontiguousarray(np.stack([np.asarray(m).reshape(DC, P).T for m in (L0_ffn_mu_r, L0_ffn_mu_k)], axis=1)),
        "ident": np.eye(P, dtype=np.float32),
        "sign": np.tile(np.repeat(np.array([1.0, -1.0], np.float32), KD), 4).reshape(P, 1),
    }
    nc = bacc.Bacc("TRN2", target_bir_lowering=False, num_devices=1)
    aps = {k: nc.dram_tensor(f"in_{k}", a.shape, mybir.dt.from_np(a.dtype), kind="ExternalInput").ap()
           for k, a in arrays.items()}
    aps["out"] = nc.dram_tensor("out", (B * N, D), F32, kind="ExternalOutput").ap()
    build(nc, **aps)
    r = run_bass_kernel_spmd(nc, [{f"in_{k}": a for k, a in arrays.items()}], core_ids=[0])
    return r.results[0]["out"].reshape(B, N, D)
```

```python
from contextlib import ExitStack

import concourse.bass as bass
from concourse import mybir

F32 = mybir.dt.float32
F32R = mybir.dt.float32r
ALU = mybir.AluOpType
ACT = mybir.ActivationFunctionType
AX_X = mybir.AxisListType.X

P = 128
B, N, D = 4, 512, 256
H, KD, VD = 16, 16, 64
L, FE = 64, 32
EPS = 1e-5
DC = D // P
NT = N // P
NP = H // 2
HALF = N // 2
STEPS = NP * NT * 2
TILES = B * STEPS
S_BANKS, AV_BANKS, MISC_BANKS = 3, 2, 3
E_RING = 8
X_RING = 3
STACK = 4
AV_LAG, SCALE_LAG = 6, 2
OE_LAG = 2 * NT + AV_LAG - 1

V_ON_DVE = (1, 3)
X_TILES = 3
BANKED = {"t1", "qk", "v", "op", "t2", "kv", "kf", "z", "xs", "pt", "pv", "fc", "t3", "fr", "fk", "fv"}

PLAN = [
    (1, "qk", 0, (1, 0)), (4, "qk_lo", 0, (1, 0)), (5, "v", 0, (1, 0)), (5, "qk", 0, (1, 1)), (7, "op", -1, (1, 0)),
    (8, "qk_lo", 0, (1, 1)), (8, "ld", 0, (3,)), (9, "ln2", -1, (0,)), (9, "ld", 0, (4,)), (9, "v", 0, (1, 1)),
    (10, "kv", -1, ()), (11, "op", -1, (1, 1)), (12, "ln2", -1, (1,)), (12, "t2", -1, (0,)), (12, "t2_lo", -1, (0,)),
    (13, "v", 0, (1, 2)), (14, "z", -1, (0, 0)), (15, "z", -1, (0, 1)), (16, "t2", -1, (1,)), (17, "xs", -1, (0, 0)),
    (17, "t2_lo", -1, (1,)), (19, "xn", -1, (0, 0)), (19, "xs", -1, (0, 1)), (20, "z", -1, (1, 0)),
    (20, "xs", -1, (1, 0)), (20, "v", 0, (1, 3)), (20, "xn", -1, (0, 1)), (21, "z", -1, (1, 1)),
    (21, "xn", -1, (1, 0)), (22, "pt", -1, (0, 0)), (23, "xs", -1, (1, 1)), (24, "xn", -1, (1, 1)),
    (24, "pt", -1, (0, 1)), (25, "pt", -1, (1, 0)), (25, "xs", -1, (2, 0)), (25, "xs", -1, (2, 1)),
    (26, "xn", -1, (2, 0)), (27, "pt", -1, (1, 1)), (27, "pv", -1, (0, 0)), (27, "xs", -1, (3, 0)),
    (27, "xn", -1, (2, 1)), (28, "pv", -1, (0, 1)), (28, "ld", 0, (5,)), (28, "pv_lo", -1, (0, 0)),
    (28, "xn", -1, (3, 0)), (28, "pv_lo", -1, (0, 1)), (29, "pt", -1, (2, 0)), (29, "xs", -1, (3, 1)),
    (30, "xn", -1, (3, 1)), (30, "fc", -1, (0,)), (31, "pt", -1, (2, 1)), (31, "pt", -1, (3, 0)),
    (31, "ln3", -1, (0,)), (32, "pt", -1, (3, 1)), (32, "ln1", 1, (0,)), (34, "pv", -1, (1, 0)),
    (34, "pv", -1, (1, 1)), (36, "ld", 0, (6,)), (36, "pv_lo", -1, (1, 0)), (36, "pv_lo", -1, (1, 1)),
    (37, "t3", -1, (0,)), (37, "ln1", 1, (1,)), (38, "mix", -1, (0,)), (38, "t1", 1, (0,)), (38, "t1_lo", 1, (0,)),
    (38, "fc", -1, (1,)), (40, "ln3", -1, (1,)), (40, "t1_lo", 1, (1,)), (40, "op", 0, (0, 0)), (40, "t1", 1, (1,)),
    (41, "fr", -1, (0,)), (41, "ld", 0, (7,)), (42, "fk", -1, (0,)), (42, "t3", -1, (1,)), (42, "qk", 1, (0, 0)),
    (42, "mix", -1, (1,)), (43, "qk_lo", 1, (0, 0)), (44, "op", 0, (0, 1)), (46, "fv", -1, (0,)),
    (46, "qk", 1, (0, 1)), (47, "v", 1, (0, 0)), (47, "qk_lo", 1, (0, 1)), (49, "fk", -1, (1,)), (51, "fr", -1, (1,)),
    (51, "ld", 1, (0,)), (52, "ld", 1, (1,)), (52, "ld", 1, (2,)), (52, "v", 1, (0, 1)), (53, "fv", -1, (1,)),
    (55, "v", 1, (0, 2)), (58, "x_load", 2, ()), (63, "v", 1, (0, 3)),
]
LAST = [
    (2, "kv", ()), (6, "op", (1, 0)), (7, "ln2", (0,)), (7, "op", (1, 1)), (14, "ln2_do", (0,)), (15, "ln2", (1,)),
    (16, "t2", (0,)), (18, "t2_lo", (0,)), (19, "ln2_do", (1,)), (19, "z", (0, 0)), (19, "t2", (1,)),
    (20, "t2_lo", (1,)), (20, "z", (0, 1)), (21, "xs", (0, 0)), (24, "xs", (0, 1)), (27, "z", (1, 0)),
    (27, "xn", (0, 0)), (27, "xn", (0, 1)), (27, "xs", (1, 0)), (27, "z", (1, 1)), (27, "xs", (1, 1)),
    (28, "xs", (2, 0)), (30, "xn", (1, 0)), (30, "xn", (1, 1)), (30, "pt", (0, 0)), (31, "pt", (0, 1)),
    (31, "xs", (2, 1)), (32, "xn", (2, 0)), (35, "pt", (1, 0)), (37, "xs", (3, 0)), (40, "pt", (1, 1)),
    (42, "xs", (3, 1)), (42, "xn", (2, 1)), (43, "pv", (0, 0)), (44, "pv", (0, 1)), (44, "pt", (2, 0)),
    (44, "pv_lo", (0, 0)), (44, "pv_lo", (0, 1)), (45, "xn", (3, 0)), (46, "xn", (3, 1)), (47, "pt", (2, 1)),
    (47, "fc", (0,)), (49, "pt", (3, 0)), (52, "pt", (3, 1)), (52, "pv", (1, 0)), (53, "pv", (1, 1)),
    (56, "ln3", (0,)), (63, "ln3_do", (0,)), (63, "pv_lo", (1, 0)), (63, "pv_lo", (1, 1)), (63, "t3", (0,)),
    (63, "mix", (0,)), (63, "fc", (1,)), (63, "ln3", (1,)), (63, "ln3_do", (1,)), (63, "fk", (0,)), (63, "mix", (1,)),
    (63, "fr", (0,)), (63, "t3", (1,)), (63, "fv", (0,)), (63, "fk", (1,)), (63, "fr", (1,)), (63, "fv", (1,)),
]
FIRST = [
    ("load", 0, ("fc",)), ("ln1", 0, (0,)), ("ln1", 0, (1,)), ("ln1_do", 0, (0,)), ("ln1_do", 0, (1,)),
    ("t1_lo", 0, (0,)), ("cut", 0, ("qk",)), ("t1", 0, (0,)), ("t1", 0, (1,)), ("t1_lo", 0, (1,)),
    ("qk_lo", 0, (0, 0)), ("cut", 0, ("v",)), ("qk", 0, (0, 0)), ("qk", 0, (0, 1)), ("qk_lo", 0, (0, 1)),
    ("ld", 0, (0,)), ("load", 0, ("o",)), ("load", 0, ("rest",)), ("load", 0, ("feat",)), ("ld", 0, (1,)),
    ("ld", 0, (2,)), ("v", 0, (0, 0)), ("v", 0, (0, 1)), ("v", 0, (0, 2)), ("v", 0, (0, 3)),
]
ONCE = [
    (1, "cut", ("fc",)), (5, "cut", ("o",)), (5, "feat", ()), (13, "kf", (0,)), (17, "kf", (1,)),
]


def schedule():
    rounds = [(-1, FIRST)]
    for r in range(B + 1):
        for step in range(STEPS):
            plan = PLAN if r < B else [(at, name, -1, args) for at, name, args in LAST]
            stages = [(name, 0, args) for at, name, args in ONCE if (r, step) == (0, at)]
            stages += [(name, r + off, args) for at, name, off, args in plan if at == step and 0 <= r + off < B]
            rounds.append((r * STEPS + step, stages))
    return rounds


def bank_uses(steps):
    uses, had = {}, [0] * (MISC_BANKS + S_BANKS)
    n = 0
    for g, stages in steps:
        ring = MISC_BANKS if 0 <= g < TILES else MISC_BANKS + S_BANKS
        for unit in stages:
            if unit[0] in BANKED:
                uses[unit] = (n % ring, had[n % ring])
                had[n % ring] += 1
                n += 1
    return uses


def banks_before_scores(steps, uses):
    units = [unit for g, stages in steps if g < 0 for unit in stages if unit[0] in BANKED]
    return [sum(uses[u][0] == MISC_BANKS + i for u in units) for i in range(S_BANKS)]


def build(nc, x, ctx_t, wqk, wv, wo, fm_t, fm_b, wfc, fc_b, wffn, mu, ident, sign, out):
    steps = schedule()
    uses = bank_uses(steps)
    used_before = banks_before_scores(steps, uses)

    with ExitStack() as ctx:
        def sb(name, shape, dt=F32):
            return ctx.enter_context(nc.sbuf_tensor(name, shape, dt))

        def sem(name):
            return ctx.enter_context(nc.semaphore(name))

        x_sb = sb("x_sb", [P, X_RING * NT, D])
        wqk_hi, wqk_lo = sb("wqk_hi", [P, DC, 2 * H * KD], F32R), sb("wqk_lo", [P, DC, 2 * H * KD], F32R)
        wv_hi, wv_lo = sb("wv_hi", [P, DC, H * VD], F32R), sb("wv_lo", [P, DC, H * VD], F32R)
        wo_hi, wo_lo = sb("wo_hi", [P, NP, D], F32R), sb("wo_lo", [P, NP, D], F32R)
        wfc_hi, wfc_lo = sb("wfc_hi", [P, 4, D], F32R), sb("wfc_lo", [P, 4, D], F32R)
        wffn_sb = sb("wffn_sb", [P, 3, DC, D])
        fm_sb = sb("fm_sb", [P, 2, 4, 2, KD])
        fm_hi, fm_lo = sb("fm_hi", [P, 2, P], F32R), sb("fm_lo", [P, 2, P], F32R)
        fmb = sb("fmb", [P, 1])
        fcb = sb("fcb", [P, D])
        mu_sb = sb("mu_sb", [P, 2, DC])
        id_sb = sb("id_sb", [P, P])
        sign_sb = sb("sign_sb", [P, 1])
        power = sb("power", [P, 2])
        xn = [sb("xn1", [P, 2, D]), sb("xn23", [P, 2, D])]
        stats = [sb("stats1", [P, 2, 6]), sb("stats23", [P, 2, 6])]
        mv = [sb("mv1", [P, 2, 2]), sb("mv23", [P, 2, 2])]
        nmean = [sb("nmean1", [P, 2, 2]), sb("nmean23", [P, 2, 2])]
        veps = [sb("veps1", [P, 2, 2]), sb("veps23", [P, 2, 2])]
        rstd = [sb("rstd1", [P, 2, 2]), sb("rstd23", [P, 2, 2])]
        xt_hi, xt_lo = sb("xt_hi", [P, DC, N], F32R), sb("xt_lo", [P, DC, N], F32R)
        qkt_hi, qkt_lo = sb("qkt_hi", [P, N], F32R), sb("qkt_lo", [P, N], F32R)
        q_st, k_st = sb("q_st", [P, STACK, N], F32R), sb("k_st", [P, STACK, N], F32R)
        v_sb = sb("v_sb", [P, NT, H, VD])
        e_sb = sb("e_sb", [P, E_RING, N])
        nmax = sb("nmax", [P, E_RING])
        esum = sb("esum", [P, 2 * E_RING])
        rsum = sb("rsum", [P, 4, 2])
        ot_hi, ot_lo = sb("ot_hi", [P, 4, N], F32R), sb("ot_lo", [P, 4, N], F32R)
        kf = sb("kf", [P, 4, B, 2, L])
        kblk = sb("kblk", [P, 4, 4, L])
        vblk = sb("vblk", [P, NP, 2 * FE])
        xt2_hi, xt2_lo = sb("xt2_hi", [P, DC, HALF], F32R), sb("xt2_lo", [P, DC, HALF], F32R)
        qf = sb("qf", [P, 4, HALF])
        sx = sb("sx", [P, X_TILES, 512])
        xmax = sb("xmax", [P, 4, 8])
        xsum = sb("xsum", [P, 4, 8])
        xrec = sb("xrec", [P, 4, 8])
        pt_sb = sb("pt_sb", [P, NP, HALF])
        oxt_hi, oxt_lo = sb("oxt_hi", [P, 4, HALF], F32R), sb("oxt_lo", [P, 4, HALF], F32R)
        xt3 = sb("xt3", [P, DC, 1 + N])
        mix_r, mix_k = sb("mix_r", [P, DC, HALF]), sb("mix_k", [P, DC, HALF])
        gate = sb("gate", [P, 2, D])
        kact = sb("kact", [P, DC, HALF])
        wqk_raw = qf[:, :, :].rearrange("p g n -> p (g n)").rearrange("p (c n) -> p c n", c=DC)
        wfc_raw = qf
        wv_raw = pt_sb[:, :, :].rearrange("p g n -> p (g n)").rearrange("p (c n) -> p c n", c=DC)
        wo_raw = v_sb[:, :, H // 2:, :].rearrange("p t h v -> p t (h v)")
        as_raw = "p (t i) n -> p t (i n)"
        ctx_sb = mix_r

        s_bank = [ctx.enter_context(nc.psum_tensor(f"s_bank{i}", [P, 512], F32)) for i in range(S_BANKS)]
        av_bank = [ctx.enter_context(nc.psum_tensor(f"av_bank{i}", [P, 512], F32)) for i in range(AV_BANKS)]
        m_bank = [ctx.enter_context(nc.psum_tensor(f"m_bank{i}", [P, 512], F32)) for i in range(MISC_BANKS)]
        m_bank += s_bank

        q_parts = nc.dram_tensor("q_parts", (2, 8, 2, KD, N), F32, kind="Internal").ap()
        k_parts = nc.dram_tensor("k_parts", (2, 8, 2, KD, 2, N), F32, kind="Internal").ap()

        x_in, x_half_in = [sem(f"x_in{b}") for b in range(B)], sem("x_half_in")
        wqk_in, wv_in, wo_in, wfc_in, id_in = (sem(f"{n}_in") for n in ("wqk", "wv", "wo", "wfc", "id"))
        fm_zero, fm_in, ctx_in, post_in = sem("fm_zero"), sem("fm_in"), sem("ctx_in"), sem("post_in")
        stack_in = [[sem(f"{o}_stack_in{i}") for i in range(STACK)] for o in "qk"]
        stack_out = [[sem(f"{o}_parts_out{c}") for c in range(2)] for o in "qk"]
        res_out = [sem(f"res_out{i}") for i in range(2)]
        filled = [sem(f"filled{i}") for i in range(MISC_BANKS + S_BANKS)]
        emptied = [sem(f"emptied{i}") for i in range(MISC_BANKS + S_BANKS)]
        consts_set, wgt_hi, wgt_lo, fm_ready, fm_cut = (
            sem("consts_set"), sem("wgt_hi"), sem("wgt_lo"), sem("fm_ready"), sem("fm_cut"))
        var_ready = [sem("var_ready1"), sem("var_ready23")]
        rstd_ready = [sem("rstd_ready1"), sem("rstd_ready23")]
        xn_ready = [sem("xn_ready1"), sem("xn_ready23")]
        dve_chain, pool_chain = sem("dve_chain"), sem("pool_chain")
        xt_hi_ready, qk_hi_ready = sem("xt_hi_ready"), sem("qk_hi_ready")
        scores_ready, nmax_ready, exp_ready = sem("scores_ready"), sem("nmax_ready"), sem("exp_ready")
        rsum_ready, v_scaled, av_done = sem("rsum_ready"), sem("v_scaled"), sem("av_done")
        ot_hi_ready, ot_ready = sem("ot_hi_ready"), sem("ot_ready")
        bias_added, kblk_ready = sem("bias_added"), sem("kblk_ready")
        xt2_hi_ready, oxt_hi_ready = sem("xt2_hi_ready"), sem("oxt_hi_ready")
        xexp_ready, xrec_ready, xp_ready = sem("xexp_ready"), sem("xrec_ready"), sem("xp_ready")
        mix_ready, relu_ready, kact_ready, res_ready = (sem("mix_ready"), sem("relu_ready"),
                                                        sem("kact_ready"), sem("res_ready"))

        block = ctx.enter_context(nc.Block())

        def bank(unit):
            return m_bank[uses[unit][0]]

        def wait_filled(eng, unit):
            i, before = uses[unit]
            eng.wait_ge(filled[i], before + 1)

        def wait_emptied(eng, unit):
            i, before = uses[unit]
            eng.wait_ge(emptied[i], before + 1)

        def wait_bank(eng, unit):
            i, before = uses[unit]
            if before:
                eng.wait_ge(emptied[i], before)
            if i >= MISC_BANKS and before == used_before[i - MISC_BANKS]:
                if before or unit[1] == B - 1:
                    eng.wait_ge(exp_ready, TILES)

        def parts_of(b, c, o):
            if (b, c, o) == (0, 0, 1):
                return ot_hi[:, 0, :], ot_lo[:, 0, :]
            return qkt_hi[:, :], qkt_lo[:, :]

        def on_vector(k, b):
            return (k, b) == (1, 0) or (k > 1 and b == B - 1)

        def apply_norm(eng, k, b, half):
            i = k > 1
            count = 2 * b + half if k == 1 else 4 * b + 2 * (k - 2) + half
            eng.wait_ge(rstd_ready[i], count + 1)
            if k == 1 and count:
                pb, ph = (b, 0) if half else (b - 1, 1)
                wait_filled(eng, ("t1", pb, (ph,)))
            elif k > 1 and count:
                pk, pb, ph = (k, b, 0) if half else (2, b, 1) if k == 3 else (3, b - 1, 1)
                wait_filled(eng, (f"t{pk}", pb, (ph,)))
            for t2 in range(2):
                ins = eng.tensor_scalar(xn[i][:, t2, :], x_sb[:, x_at(b, half) + t2, :],
                                        nmean[i][:, count % 2, t2:t2 + 1], rstd[i][:, count % 2, t2:t2 + 1],
                                        ALU.add, ALU.mult)
            ins.then_inc(xn_ready[i], 1)

        def x_tile(n):
            return e_sb[:, n % 8, :] if n >= 8 * (B - 1) else sx[:, n % X_TILES, :]

        def x_at(b, half):
            return b % X_RING * NT + 2 * half

        def lagged(g):
            scale = (g - SCALE_LAG) // 2 if g >= SCALE_LAG and (g - SCALE_LAG) % 2 == 0 else None
            weigh = (g - AV_LAG) // 2 if g >= AV_LAG and (g - AV_LAG) % 2 == 0 else None
            high = (g - OE_LAG) // 8 if g >= OE_LAG and (g - OE_LAG) % 8 == 0 else None
            keep = lambda n, top: n if n is not None and n < top else None
            return keep(scale, TILES // 2), keep(weigh, TILES // 2), keep(high, B * NP)

        @block.sync
        def _(sp):
            xv = x.rearrange("(t p) d -> p t d", p=P)
            for half in range(2):
                sp.dma_start(x_sb[:, 2 * half:2 * half + 2, :], xv[:, 2 * half:2 * half + 2, :])\
                  .then_inc((x_in[0], x_half_in)[half], 16)
            sp.dma_start(wqk_raw, wqk).then_inc(wqk_in, 16)
            sp.dma_start(id_sb[:], ident).then_inc(id_in, 16)
            sp.dma_start(wv_raw, wv).then_inc(wv_in, 16)

            def load(b, what):
                if what == "o":
                    sp.dma_start(wo_raw, wo.rearrange(as_raw, i=2)).then_inc(wo_in, 16)
                elif what == "fc":
                    sp.wait_ge(wgt_lo, 1)
                    sp.dma_start(wfc_raw[:], wfc).then_inc(wfc_in, 16)
                elif what == "feat":
                    sp.dma_start(ctx_sb[:], ctx_t).then_inc(ctx_in, 16)
                    sp.dma_start(sign_sb[:], sign).then_inc(fm_in, 16)
                    sp.dma_start(fmb[:, :], bass.AP(fm_b.tensor, 0, [[0, 8], [1, KD], [1, 1]])).then_inc(fm_in, 16)
                    sp.wait_ge(fm_zero, 1)
                    for h in range(8):
                        sp.dma_start(fm_sb[h * KD:(h + 1) * KD, h // 4, h % 4, :, :],
                                     bass.AP(fm_t.tensor, 0, [[KD, KD], [0, 2], [1, KD]])).then_inc(fm_in, 16)
                else:
                    for n in range(1, X_RING):
                        sp.dma_start(x_sb[:, n * NT:(n + 1) * NT, :], xv[:, n * NT:(n + 1) * NT, :]).then_inc(x_in[n], 16)
                    sp.dma_start(fcb[:], fc_b.partition_broadcast(P)).then_inc(post_in, 16)
                    sp.dma_start(mu_sb[:], mu).then_inc(post_in, 16)
                    sp.dma_start(wffn_sb[:], wffn).then_inc(post_in, 16)

            def qk_lo(b, c, o):
                wait_emptied(sp, ("qk", b, (c, o)))
                if b:
                    for i in range(STACK):
                        sp.wait_ge(stack_in[o][i], 16 * ((b - 1) * 2 + c + 1))
                for part in range(2):
                    src = parts_of(b, c, o)[part].bitcast(F32)
                    if o == 0:
                        sp.dma_start(q_parts[c, :, part], src).then_inc(stack_out[o][c], 16)
                    else:
                        for twice in range(2):
                            sp.dma_start(k_parts[c, :, twice, :, part], src).then_inc(stack_out[o][c], 16)

            def ld(b, p):
                n = b * NP + p
                c, h = p // 4, 2 * (p % 4)
                rows = [bass.AP(q_parts.tensor, q_parts[c, h].offset, [[N, P // 2], [0, 2], [1, N]]),
                        k_parts[c, h:h + 2].rearrange("h t k i n -> (h t k i) n")]
                for o, st in ((0, q_st), (1, k_st)):
                    sp.wait_ge(stack_out[o][c], (32, 64)[o] * (b + 1))
                    if n >= STACK and o == 0:
                        sp.wait_ge(scores_ready, 8 * (n - STACK + 1))
                    sp.dma_start(st[:, n % STACK, :].bitcast(F32), rows[o]).then_inc(stack_in[o][n % STACK], 16)

            def fv(b, half):
                sp.wait_ge(res_ready, 2 * b + half + 1)
                t, at = b * NT + 2 * half, x_at(b, half)
                sp.dma_start(out.rearrange("(t p) d -> p t d", p=P)[:, t:t + 2, :],
                             x_sb[:, at:at + 2, :]).then_inc(res_out[half], 16)

            def x_load(b):
                if b >= X_RING:
                    for half in range(2):
                        sp.wait_ge(res_out[half], 16 * (b - X_RING + 1))
                    sp.dma_start(x_sb[:, x_at(b, 0):x_at(b, 0) + NT, :], xv[:, b * NT:(b + 1) * NT, :])\
                      .then_inc(x_in[b], 16)

            parts = {"load": load, "x_load": x_load, "qk_lo": qk_lo, "ld": ld, "fv": fv}
            for g, stages in steps:
                for name, b, args in stages:
                    if name in parts:
                        parts[name](b, *args)
            for half in range(2):
                sp.wait_ge(res_out[half], 16 * B)

        @block.tensor
        def _(pe):
            def matmul3(dst, a_hi, a_lo, b_hi, b_lo, first, last):
                pe.matmul(dst, a_hi, b_hi, start=first, stop=False)
                pe.matmul(dst, a_lo, b_hi, start=False, stop=False)
                return pe.matmul(dst, a_hi, b_lo, start=False, stop=last)

            def scores(g):
                n, j = g // 8, g % 8
                m, par = j // 2, j % 2
                if j == 0:
                    pe.wait_ge(stack_in[0][n % STACK], 16 * (n // STACK + 1))
                    pe.wait_ge(stack_in[1][n % STACK], 16 * (n // STACK + 1))
                if g >= S_BANKS:
                    pe.wait_ge(exp_ready, g - S_BANKS + 1)
                elif used_before[g]:
                    pe.wait_ge(emptied[MISC_BANKS + g], used_before[g])
                rows = slice(64 * par, 64 * par + 64)
                pe.matmul(s_bank[g % S_BANKS][:, :], k_st[rows, n % STACK, m * P:(m + 1) * P],
                          q_st[rows, n % STACK, :], start=True, stop=True).then_inc(scores_ready, 1)

            def weigh(n):
                m, p = n % NT, (n // NT) % NP
                if m == 0 and n // NT >= AV_BANKS:
                    pe.wait_ge(ot_ready, n // NT - AV_BANKS + 1)
                pe.wait_ge(v_scaled, n + 1)
                for par in range(2):
                    mm = pe.matmul(av_bank[n // NT % AV_BANKS][64 * par:64 * par + 64, :], v_sb[:, m, 2 * p + par, :],
                                   e_sb[:, (2 * n + par) % E_RING, :], start=(m == 0), stop=(m == NT - 1))
                mm.then_inc(av_done, 1)

            def transposed(k):
                def t(b, half):
                    unit = (f"t{k}", b, (half,))
                    wait_bank(pe, unit)
                    i = k > 1
                    count = 2 * b + half if k == 1 else 4 * b + 2 * (k - 2) + half
                    pe.wait_ge(xn_ready[i], count + 1)
                    if unit == ("t1", 0, (0,)):
                        pe.wait_ge(id_in, 16)
                    for c in range(DC):
                        for t2 in range(2):
                            mm = pe.transpose(bank(unit)[:, c * HALF + t2 * P:c * HALF + (t2 + 1) * P],
                                              xn[i][:, t2, c * P:(c + 1) * P], id_sb[:, :])
                    mm.then_inc(filled[uses[unit][0]], 1)
                return t

            def qk(b, c, o):
                unit = ("qk", b, (c, o))
                wait_bank(pe, unit)
                for half in range(2):
                    wait_emptied(pe, ("t1", b, (half,)))
                if b == 0:
                    pe.wait_ge(wgt_lo, 1)
                cols = slice(o * D + c * P, o * D + (c + 1) * P)
                for d in range(DC):
                    mm = matmul3(bank(unit)[:, :], wqk_hi[:, d, cols], wqk_lo[:, d, cols],
                                 xt_hi[:, d, :], xt_lo[:, d, :], d == 0, d == DC - 1)
                mm.then_inc(filled[uses[unit][0]], 1)

            def v(b, hh, m):
                unit = ("v", b, (hh, m))
                wait_bank(pe, unit)
                wait_emptied(pe, ("t1", b, (m // 2,)))
                if b == 0:
                    pe.wait_ge(wgt_lo, 2)
                for d in range(DC):
                    mm = matmul3(bank(unit)[:, :], xt_hi[:, d, m * P:(m + 1) * P], xt_lo[:, d, m * P:(m + 1) * P],
                                 wv_hi[:, d, hh * 512:(hh + 1) * 512], wv_lo[:, d, hh * 512:(hh + 1) * 512],
                                 d == 0, d == DC - 1)
                mm.then_inc(filled[uses[unit][0]], 1)

            def op(b, hh, tt):
                unit = ("op", b, (hh, tt))
                wait_bank(pe, unit)
                pe.wait_ge(ot_ready, b * NP + 4 * hh + 4)
                if b == 0 and hh == 0:
                    pe.wait_ge(wgt_lo, 4)
                for t2 in range(2):
                    at = (2 * tt + t2) * P
                    for p in range(4):
                        mm = matmul3(bank(unit)[:, t2 * D:(t2 + 1) * D], ot_hi[:, p, at:at + P], ot_lo[:, p, at:at + P],
                                     wo_hi[:, 4 * hh + p, :], wo_lo[:, 4 * hh + p, :], p == 0, p == 3)
                mm.then_inc(filled[uses[unit][0]], 1)

            def kf_(b, gg):
                unit = ("kf", b, (gg,))
                wait_bank(pe, unit)
                pe.wait_ge(fm_ready, 1)
                pe.wait_ge(ctx_in, 16)
                for i in range(2):
                    mm = pe.matmul(bank(unit)[:, i * HALF:(i + 1) * HALF],
                                   fm_sb[:, i].rearrange("p h s e -> p (h s e)"), ctx_sb[:, gg, :],
                                   start=True, stop=True)
                mm.then_inc(filled[uses[unit][0]], 1)

            def kv(b):
                unit = ("kv", b, ())
                wait_bank(pe, unit)
                for gg in range(2):
                    wait_emptied(pe, ("kf", 0, (gg,)))
                for i in range(4):
                    mm = pe.transpose(bank(unit)[:, i * P:(i + 1) * P], kf[:, i, b].rearrange("p r l -> p (r l)"),
                                      id_sb[:, :])
                mm.then_inc(filled[uses[unit][0]], 1)

            def z(b, half, gg):
                unit = ("z", b, (half, gg))
                wait_bank(pe, unit)
                wait_emptied(pe, ("t2", b, (half,)))
                if b == 0:
                    pe.wait_ge(fm_cut, 2)
                for i in range(2):
                    mm = matmul3(bank(unit)[:, i * HALF:(i + 1) * HALF], fm_hi[:, i], fm_lo[:, i],
                                 xt2_hi[:, gg, :], xt2_lo[:, gg, :], True, True)
                mm.then_inc(filled[uses[unit][0]], 1)

            def xs(b, t, gg):
                unit = ("xs", b, (t, gg))
                wait_bank(pe, unit)
                wait_emptied(pe, ("z", b, (t // 2, gg)))
                if t == 0:
                    pe.wait_ge(kblk_ready, b + 1)
                for i in range(2):
                    mm = pe.matmul(bank(unit)[:, i * HALF:(i + 1) * HALF],
                                   qf[:, 2 * gg + i, (t % 2) * P:(t % 2 + 1) * P],
                                   kblk[:, 2 * gg + i].rearrange("p h l -> p (h l)"), start=True, stop=True)
                mm.then_inc(filled[uses[unit][0]], 1)

            def pt(b, t, gg):
                unit = ("pt", b, (t, gg))
                wait_bank(pe, unit)
                n = 8 * b + 2 * t + gg
                pe.wait_ge(xp_ready, n + 1)
                for i in range(4):
                    mm = pe.transpose(bank(unit)[:, i * P:(i + 1) * P], x_tile(n)[:, i * P:(i + 1) * P], id_sb[:, :])
                mm.then_inc(filled[uses[unit][0]], 1)

            def pv(b, half, gg):
                unit = ("pv", b, (half, gg))
                wait_bank(pe, unit)
                for t in (2 * half, 2 * half + 1):
                    wait_emptied(pe, ("pt", b, (t, gg)))
                wait_emptied(pe, ("kv", b, ()))
                for i in range(2):
                    for q in range(2):
                        pair = 4 * gg + 2 * i + q
                        mm = pe.matmul(bank(unit)[64 * q:64 * q + 64, i * HALF:(i + 1) * HALF], vblk[:, pair, :],
                                       pt_sb[:, pair, :], start=True, stop=True)
                mm.then_inc(filled[uses[unit][0]], 1)

            def fc(b, half):
                unit = ("fc", b, (half,))
                wait_bank(pe, unit)
                for gg in range(2):
                    wait_emptied(pe, ("pv", b, (half, gg)))
                if b == 0:
                    pe.wait_ge(post_in, 48)
                for t2 in range(2):
                    for i in range(4):
                        at = slice(t2 * P, (t2 + 1) * P)
                        mm = matmul3(bank(unit)[:, t2 * D:(t2 + 1) * D], oxt_hi[:, i, at], oxt_lo[:, i, at],
                                     wfc_hi[:, i, :], wfc_lo[:, i, :], i == 0, i == 3)
                mm.then_inc(filled[uses[unit][0]], 1)

            def fr(b, half):
                unit = ("fr", b, (half,))
                wait_bank(pe, unit)
                pe.wait_ge(mix_ready, 2 * b + half + 1)
                for t2 in range(2):
                    for c in range(DC):
                        mm = pe.matmul(bank(unit)[:, t2 * D:(t2 + 1) * D], mix_r[:, c, t2 * P:(t2 + 1) * P],
                                       wffn_sb[:, 0, c, :], start=(c == 0), stop=(c == DC - 1))
                mm.then_inc(filled[uses[unit][0]], 1)

            def fk(b, half):
                unit = ("fk", b, (half,))
                wait_bank(pe, unit)
                pe.wait_ge(mix_ready, 2 * b + half + 1)
                for mc in range(DC):
                    for c in range(DC):
                        mm = pe.matmul(bank(unit)[:, mc * HALF:(mc + 1) * HALF],
                                       wffn_sb[:, 1, c, mc * P:(mc + 1) * P], mix_k[:, c, :],
                                       start=(c == 0), stop=(c == DC - 1))
                mm.then_inc(filled[uses[unit][0]], 1)

            def fv(b, half):
                unit = ("fv", b, (half,))
                wait_bank(pe, unit)
                pe.wait_ge(kact_ready, 2 * b + half + 1)
                for t2 in range(2):
                    for c in range(DC):
                        mm = pe.matmul(bank(unit)[:, t2 * D:(t2 + 1) * D], kact[:, c, t2 * P:(t2 + 1) * P],
                                       wffn_sb[:, 2, c, :], start=(c == 0), stop=(c == DC - 1))
                mm.then_inc(filled[uses[unit][0]], 1)

            parts = {"t1": transposed(1), "t2": transposed(2), "t3": transposed(3), "qk": qk, "v": v, "op": op,
                     "kf": kf_, "kv": kv, "z": z, "xs": xs, "pt": pt, "pv": pv, "fc": fc, "fr": fr, "fk": fk, "fv": fv}
            for g, stages in steps:
                if 0 <= g < TILES:
                    scores(g)
                _, n, _ = lagged(g)
                if n is not None:
                    weigh(n)
                for name, b, args in stages:
                    if name in parts:
                        parts[name](b, *args)

        @block.scalar
        def _(act):
            def exponentials(g):
                act.wait_ge(nmax_ready, g + 1)
                if g >= E_RING:
                    act.wait_ge(av_done, (g - E_RING) // 2 + 1)
                act.activation(e_sb[:, g % E_RING, :], s_bank[g % S_BANKS][:, :], ACT.Exp,
                               bias=nmax[:, g % E_RING:g % E_RING + 1],
                               accum_out=esum[:, g % (2 * E_RING):g % (2 * E_RING) + 1]).then_inc(exp_ready, 1)

            def ot_high(n):
                act.wait_ge(av_done, NT * (n + 1))
                if n >= 4:
                    last = (n // 4 - 1)
                    wait_filled(act, ("op", last // 2, (last % 2, 1)))
                elif n == 0:
                    act.wait_ge(stack_out[1][0], 64)
                act.activation(ot_hi[:, n % 4, :], av_bank[n % AV_BANKS][:, :], ACT.Copy).then_inc(ot_hi_ready, 1)

            def cut(b, which):
                if which == "qk":
                    act.wait_ge(wqk_in, 16)
                    act.activation(wqk_hi[:, :, 0:D], wqk_raw[:, :, 0:D], ACT.Copy, scale=KD ** -0.5)
                    act.activation(wqk_hi[:, :, D:], wqk_raw[:, :, D:], ACT.Copy).then_inc(wgt_hi, 1)
                elif which == "v":
                    act.wait_ge(wv_in, 16)
                    act.activation(wv_hi[:, :, :], wv_raw, ACT.Copy).then_inc(wgt_hi, 1)
                elif which == "fc":
                    act.wait_ge(wfc_in, 16)
                    act.activation(wfc_hi[:, :, :], wfc_raw[:, :, :], ACT.Copy).then_inc(wgt_hi, 1)
                else:
                    act.wait_ge(wo_in, 16)
                    act.activation(wo_hi[:, :, :].rearrange(as_raw, i=2), wo_raw, ACT.Copy).then_inc(wgt_hi, 1)

            def feat(b):
                act.wait_ge(fm_ready, 1)
                act.activation(fm_hi[:, :, :], fm_sb[:, :, :, :, :].rearrange("p g h s e -> p g (h s e)"), ACT.Copy)\
                   .then_inc(fm_cut, 1)

            def t1(b, half):
                unit = ("t1", b, (half,))
                wait_filled(act, unit)
                if b:
                    wait_filled(act, ("v", b - 1, (1, NT - 1)))
                    wait_filled(act, ("qk", b - 1, (1, 1)))
                act.activation(xt_hi[:, :, half * HALF:(half + 1) * HALF],
                               bank(unit)[:, :].rearrange("p (c n) -> p c n", c=DC), ACT.Copy).then_inc(xt_hi_ready, 1)

            def qk(b, c, o):
                unit = ("qk", b, (c, o))
                wait_filled(act, unit)
                n = 4 * b + 2 * c + o
                if n >= 2:
                    before = n - 1 if n > 2 else 0
                    act.wait_ge(stack_out[before % 2][before // 2 % 2], (32, 64)[before % 2] * (before // 4 + 1))
                act.activation(parts_of(b, c, o)[0], bank(unit)[:, :], ACT.Copy).then_inc(qk_hi_ready, 1)

            def v(b, hh, m):
                if m not in V_ON_DVE:
                    unit = ("v", b, (hh, m))
                    wait_filled(act, unit)
                    if b == 0 and hh:
                        act.wait_ge(wgt_lo, 4)
                    if b:
                        act.wait_ge(av_done, NT * ((b - 1) * NP + 4 * hh + 4))
                    act.activation(v_sb[:, m, 8 * hh:8 * hh + 8, :],
                                   bank(unit)[:, :].rearrange("p (h v) -> p h v", h=8), ACT.Copy)\
                       .then_inc(emptied[uses[unit][0]], 1)

            def kf_(b, gg):
                unit = ("kf", b, (gg,))
                wait_filled(act, unit)
                for twice in range(2):
                    for i in range(2):
                        ins = act.activation(kf[:, 2 * gg + i, :, twice, :],
                                             bank(unit)[:, i * HALF:(i + 1) * HALF].rearrange("p (b l) -> p b l", b=B),
                                             ACT.Exp, bias=fmb[:, 0:1])
                ins.then_inc(emptied[uses[unit][0]], 1)

            def t2(b, half):
                unit = ("t2", b, (half,))
                wait_filled(act, unit)
                if (b, half) != (0, 0):
                    pb, ph = (b, 0) if half else (b - 1, 1)
                    wait_filled(act, ("z", pb, (ph, 1)))
                act.activation(xt2_hi[:, :, :], bank(unit)[:, :].rearrange("p (c n) -> p c n", c=DC), ACT.Copy)\
                   .then_inc(xt2_hi_ready, 1)

            def z(b, half, gg):
                unit = ("z", b, (half, gg))
                wait_filled(act, unit)
                if (b, half) != (0, 0):
                    pb, ph = (b, 0) if half else (b - 1, 1)
                    wait_filled(act, ("xs", pb, (2 * ph + 1, gg)))
                act.activation(qf[:, 2 * gg:2 * gg + 2, :], bank(unit)[:, :].rearrange("p (g n) -> p g n", g=2),
                               ACT.Exp, bias=fmb[:, 0:1]).then_inc(emptied[uses[unit][0]], 1)

            def xs(b, t, gg):
                n = 8 * b + 2 * t + gg
                wait_emptied(act, ("xs", b, (t, gg)))
                act.activation(x_tile(n), x_tile(n), ACT.Exp).then_inc(xexp_ready, 1)

            def pt(b, t, gg):
                unit = ("pt", b, (t, gg))
                wait_filled(act, unit)
                if (b, t) >= (0, 2):
                    pb, ph = (b, 0) if t >= 2 else (b - 1, 1)
                    wait_filled(act, ("pv", pb, (ph, gg)))
                act.activation(pt_sb[:, 4 * gg:4 * gg + 4, (t % 2) * P:(t % 2 + 1) * P],
                               bank(unit)[:, :].rearrange("p (i n) -> p i n", i=4), ACT.Copy)\
                   .then_inc(emptied[uses[unit][0]], 1)

            def pv(b, half, gg):
                unit = ("pv", b, (half, gg))
                wait_filled(act, unit)
                if (b, half) != (0, 0):
                    pb, ph = (b, 0) if half else (b - 1, 1)
                    wait_filled(act, ("fc", pb, (ph,)))
                act.activation(oxt_hi[:, 2 * gg:2 * gg + 2, :], bank(unit)[:, :].rearrange("p (i n) -> p i n", i=2),
                               ACT.Copy).then_inc(oxt_hi_ready, 1)

            def t3(b, half):
                unit = ("t3", b, (half,))
                wait_filled(act, unit)
                if b and half == 0:
                    act.wait_ge(mix_ready, 2 * b)
                act.activation(xt3[:, :, 1 + half * HALF:1 + (half + 1) * HALF],
                               bank(unit)[:, :].rearrange("p (c n) -> p c n", c=DC), ACT.Copy)\
                   .then_inc(emptied[uses[unit][0]], 1)

            def fr(b, half):
                unit = ("fr", b, (half,))
                wait_filled(act, unit)
                n = 2 * b + half
                if n:
                    act.wait_ge(res_ready, n)
                act.activation(gate[:, :, :], bank(unit)[:, :].rearrange("p (t d) -> p t d", t=2), ACT.Tanh,
                               scale=0.5).then_inc(emptied[uses[unit][0]], 1)

            def fk(b, half):
                unit = ("fk", b, (half,))
                wait_filled(act, unit)
                if (b, half) != (0, 0):
                    pb, ph = (b, 0) if half else (b - 1, 1)
                    wait_filled(act, ("fv", pb, (ph,)))
                act.activation(kact[:, :, :], bank(unit)[:, :].rearrange("p (c n) -> p c n", c=DC), ACT.Relu)\
                   .then_inc(emptied[uses[unit][0]], 1)

            parts = {"cut": cut, "feat": feat, "t1": t1, "qk": qk, "v": v, "kf": kf_, "t2": t2, "z": z, "xs": xs, "pt": pt,
                     "pv": pv, "t3": t3, "fr": fr, "fk": fk}
            for g, stages in steps:
                _, _, n = lagged(g)
                if n is not None:
                    ot_high(n)
                if 0 <= g < TILES:
                    exponentials(g)
                for name, b, args in stages:
                    if name in parts:
                        parts[name](b, *args)

        @block.vector
        def _(dve):
            chained = [0]

            def link(ins):
                chained[0] += 1
                ins.then_inc(dve_chain, 1)
                dve.wait_ge(dve_chain, chained[0])

            dve.memset(vblk[:, :, :], 0.0).then_inc(consts_set, 1)

            def maxima(g):
                dve.wait_ge(scores_ready, g + 1)
                dve.tensor_reduce(nmax[:, g % E_RING:g % E_RING + 1], s_bank[g % S_BANKS][:, :], AX_X, ALU.max,
                                  negate=True).then_inc(nmax_ready, 1)

            def row_sums(n):
                dve.wait_ge(exp_ready, 2 * n + 2)
                at = (2 * n) % (2 * E_RING)
                if n >= 4:
                    dve.wait_ge(v_scaled, n - 3)
                dve.reciprocal(rsum[:, n % 4, :], esum[:, at:at + 2]).then_inc(rsum_ready, 1)

            def ot_low(n):
                dve.wait_ge(ot_hi_ready, n + 1)
                dve.tensor_tensor(ot_lo[:, n % 4, :], av_bank[n % AV_BANKS][:, :], ot_hi[:, n % 4, :].bitcast(F32), ALU.subtract)\
                   .then_inc(ot_ready, 1)

            def cut(b, which):
                if which == "qk":
                    dve.wait_ge(wgt_hi, 1)
                    dve.scalar_tensor_tensor(out=wqk_lo[:, :, 0:D], in0=wqk_raw[:, :, 0:D], scalar=KD ** -0.5,
                                             in1=wqk_hi[:, :, 0:D].bitcast(F32), op0=ALU.mult, op1=ALU.subtract)
                    dve.tensor_tensor(wqk_lo[:, :, D:], wqk_raw[:, :, D:], wqk_hi[:, :, D:].bitcast(F32),
                                      ALU.subtract).then_inc(wgt_lo, 1)
                elif which == "v":
                    dve.wait_ge(wgt_hi, 2)
                    dve.tensor_tensor(wv_lo[:, :, :], wv_raw, wv_hi[:, :, :].bitcast(F32), ALU.subtract)\
                       .then_inc(wgt_lo, 1)
                elif which == "fc":
                    dve.wait_ge(wgt_hi, 3)
                    dve.tensor_tensor(wfc_lo[:, :, :], wfc_raw[:, :, :], wfc_hi[:, :, :].bitcast(F32), ALU.subtract)\
                       .then_inc(wgt_lo, 1)
                else:
                    dve.wait_ge(wgt_hi, 4)
                    dve.tensor_tensor(wo_lo[:, :, :].rearrange(as_raw, i=2), wo_raw,
                                      wo_hi[:, :, :].bitcast(F32).rearrange(as_raw, i=2), ALU.subtract)\
                       .then_inc(wgt_lo, 1)

            def norm_stats(k):
                def ln(b, half):
                    i = k > 1
                    count = 2 * b + half if k == 1 else 4 * b + 2 * (k - 2) + half
                    if k == 1:
                        dve.wait_ge(x_half_in if (b, half) == (0, 1) else x_in[b], 16)
                    elif k == 2:
                        wait_emptied(dve, ("op", b, (1, half)))
                    else:
                        wait_emptied(dve, ("fc", b, (half,)))
                    if count >= 2:
                        dve.wait_ge(xn_ready[i], count - 1)
                    for t2 in range(2):
                        ins = dve.bn_stats(stats[i][:, t2, :], x_sb[:, x_at(b, half) + t2, :])
                    link(ins)
                    for t2 in range(2):
                        ins = dve.bn_aggr(mv[i][:, t2, :], stats[i][:, t2, :])
                    link(ins)
                    dve.tensor_scalar(nmean[i][:, count % 2, :], mv[i][:, :, 0], -1.0, None, ALU.mult)
                    dve.tensor_scalar(veps[i][:, count % 2, :], mv[i][:, :, 1], EPS, None, ALU.add).then_inc(var_ready[i], 1)
                return ln

            def apply_on_vector(k):
                def ln_do(b, half):
                    apply_norm(dve, k, b, half)
                return ln_do

            def t1_lo(b, half):
                unit = ("t1", b, (half,))
                dve.wait_ge(xt_hi_ready, 2 * b + half + 1)
                at = slice(half * HALF, (half + 1) * HALF)
                dve.tensor_tensor(xt_lo[:, :, at], bank(unit)[:, :].rearrange("p (c n) -> p c n", c=DC),
                                  xt_hi[:, :, at].bitcast(F32), ALU.subtract).then_inc(emptied[uses[unit][0]], 1)

            def qk_lo(b, c, o):
                unit = ("qk", b, (c, o))
                dve.wait_ge(qk_hi_ready, 4 * b + 2 * c + o + 1)
                hi, lo = parts_of(b, c, o)
                dve.tensor_tensor(lo, bank(unit)[:, :], hi.bitcast(F32), ALU.subtract)\
                   .then_inc(emptied[uses[unit][0]], 1)

            def v(b, hh, m):
                if m in V_ON_DVE:
                    unit = ("v", b, (hh, m))
                    wait_filled(dve, unit)
                    if b == 0 and hh:
                        dve.wait_ge(wgt_lo, 4)
                    if b:
                        dve.wait_ge(av_done, NT * ((b - 1) * NP + 4 * hh + 4))
                    dve.tensor_copy(v_sb[:, m, 8 * hh:8 * hh + 8, :],
                                    bank(unit)[:, :].rearrange("p (h v) -> p h v", h=8))\
                       .then_inc(emptied[uses[unit][0]], 1)

            def op(b, hh, tt):
                unit = ("op", b, (hh, tt))
                wait_filled(dve, unit)
                at = x_at(b, tt)
                if hh:
                    wait_emptied(dve, ("op", b, (0, tt)))
                dve.tensor_tensor(x_sb[:, at:at + 2, :], bank(unit)[:, :].rearrange("p (t d) -> p t d", t=2),
                                  x_sb[:, at:at + 2, :], ALU.add).then_inc(emptied[uses[unit][0]], 1)

            def feat(b):
                dve.wait_ge(fm_in, 16 * 10)
                dve.tensor_scalar(fm_sb[:, :, :, 1, :].rearrange("p g h e -> p (g h) e"),
                                  fm_sb[:, :, :, 1, :].rearrange("p g h e -> p (g h) e"), -1.0, None, ALU.mult)
                dve.tensor_tensor(fmb[:, :], fmb[:, :], sign_sb[:, :], ALU.mult).then_inc(fm_ready, 1)
                dve.wait_ge(fm_cut, 1)
                dve.tensor_tensor(fm_lo[:, :, :], fm_sb[:, :, :, :, :].rearrange("p g h s e -> p g (h s e)"),
                                  fm_hi[:, :, :].bitcast(F32), ALU.subtract).then_inc(fm_cut, 1)

            def t2_lo(b, half):
                unit = ("t2", b, (half,))
                dve.wait_ge(xt2_hi_ready, 2 * b + half + 1)
                dve.tensor_tensor(xt2_lo[:, :, :], bank(unit)[:, :].rearrange("p (c n) -> p c n", c=DC),
                                  xt2_hi[:, :, :].bitcast(F32), ALU.subtract).then_inc(emptied[uses[unit][0]], 1)

            def pv_lo(b, half, gg):
                unit = ("pv", b, (half, gg))
                dve.wait_ge(oxt_hi_ready, 4 * b + 2 * half + gg + 1)
                at = slice(2 * gg, 2 * gg + 2)
                dve.tensor_tensor(oxt_lo[:, at, :], bank(unit)[:, :].rearrange("p (i n) -> p i n", i=2),
                                  oxt_hi[:, at, :].bitcast(F32), ALU.subtract).then_inc(emptied[uses[unit][0]], 1)

            def kv(b):
                unit = ("kv", b, ())
                wait_filled(dve, unit)
                if b:
                    wait_filled(dve, ("xs", b - 1, (NT - 1, 0)))
                    wait_filled(dve, ("xs", b - 1, (NT - 1, 1)))
                else:
                    dve.wait_ge(consts_set, 2)
                for h in range(4):
                    ins = dve.tensor_scalar(kblk[32 * h:32 * h + 32, :, h, :], kf[32 * h:32 * h + 32, :, b, 0, :],
                                            D ** -0.5, None, ALU.mult)
                ins.then_inc(kblk_ready, 1)
                if b:
                    wait_filled(dve, ("pv", b - 1, (1, 1)))
                v4 = bank(unit)[:, :].rearrange("p (r q s) -> p r q s", q=2, s=FE)
                for q in range(2):
                    ins = dve.tensor_copy(vblk[64 * q:64 * q + 64, :, q * FE:(q + 1) * FE],
                                          v4[64 * q:64 * q + 64, :, q, :])
                ins.then_inc(emptied[uses[unit][0]], 1)

            def xs(b, t, gg):
                unit = ("xs", b, (t, gg))
                wait_filled(dve, unit)
                n = 8 * b + 2 * t + gg
                src = bank(unit)[:, :].rearrange("p (h l) -> p h l", h=8)
                link(dve.tensor_reduce(xmax[:, n % 4, :], src, AX_X, ALU.max, negate=True))
                if X_TILES <= n < 8 * (B - 1):
                    pb, r = (n - X_TILES) // 8, (n - X_TILES) % 8
                    wait_filled(dve, ("pt", pb, (r // 2, r % 2)))
                dve.tensor_tensor(x_tile(n).rearrange("p (h l) -> p h l", h=8), src,
                                  xmax[:, n % 4, :].unsqueeze(2).broadcast_to([P, 8, L]), ALU.add)\
                   .then_inc(emptied[uses[unit][0]], 1)

            def xn_(b, t, gg):
                n = 8 * b + 2 * t + gg
                dve.wait_ge(xexp_ready, n + 1)
                link(dve.tensor_reduce(xsum[:, n % 4, :], x_tile(n).rearrange("p (h l) -> p h l", h=8),
                                       AX_X, ALU.add))
                if n >= 4:
                    dve.wait_ge(xp_ready, n - 3)
                dve.reciprocal(xrec[:, n % 4, :], xsum[:, n % 4, :]).then_inc(xrec_ready, 1)

            def fc(b, half):
                unit = ("fc", b, (half,))
                wait_filled(dve, unit)
                dve.wait_ge(bias_added, 2 * b + half + 1)
                at = x_at(b, half)
                dve.tensor_tensor(x_sb[:, at:at + 2, :], bank(unit)[:, :].rearrange("p (t d) -> p t d", t=2),
                                  x_sb[:, at:at + 2, :], ALU.add).then_inc(emptied[uses[unit][0]], 1)

            def mix(b, half):
                wait_emptied(dve, ("t3", b, (half,)))
                n = 2 * b + half
                if n == 0:
                    dve.wait_ge(post_in, 48)
                if n:
                    pb, ph = (b, 0) if half else (b - 1, 1)
                    wait_filled(dve, ("fr", pb, (ph,)))
                    wait_filled(dve, ("fk", pb, (ph,)))
                cur = xt3[:, :, 1 + half * HALF:1 + (half + 1) * HALF]
                prev = xt3[:, :, half * HALF:(half + 1) * HALF]
                link(dve.tensor_tensor(mix_k[:, :, :], cur, prev, ALU.subtract))
                for c in range(DC):
                    ins = dve.scalar_tensor_tensor(out=mix_r[:, c, :], in0=mix_k[:, c, :], scalar=mu_sb[:, 0, c:c + 1],
                                                   in1=prev[:, c, :], op0=ALU.mult, op1=ALU.add)
                link(ins)
                for c in range(DC):
                    ins = dve.scalar_tensor_tensor(out=mix_k[:, c, :], in0=mix_k[:, c, :], scalar=mu_sb[:, 1, c:c + 1],
                                                   in1=prev[:, c, :], op0=ALU.mult, op1=ALU.add)
                ins.then_inc(mix_ready, 1)

            def fk(b, half):
                if b == B - 1:
                    wait_emptied(dve, ("fk", b, (half,)))
                    dve.tensor_tensor(kact[:, :, :], kact[:, :, :], kact[:, :, :], ALU.mult).then_inc(kact_ready, 1)

            def fv(b, half):
                unit = ("fv", b, (half,))
                wait_filled(dve, unit)
                wait_emptied(dve, ("fr", b, (half,)))
                at = x_at(b, half)
                dve.scalar_tensor_tensor(out=gate[:, :, :], in0=gate[:, :, :], scalar=1.0,
                                         in1=bank(unit)[:, :].rearrange("p (t d) -> p t d", t=2),
                                         op0=ALU.add, op1=ALU.mult).then_inc(emptied[uses[unit][0]], 1)
                wait_emptied(dve, unit)
                dve.scalar_tensor_tensor(out=x_sb[:, at:at + 2, :], in0=gate[:, :, :], scalar=0.5,
                                         in1=x_sb[:, at:at + 2, :], op0=ALU.mult, op1=ALU.add).then_inc(res_ready, 1)

            parts = {"cut": cut, "ln1": norm_stats(1), "ln2": norm_stats(2), "ln3": norm_stats(3),
                     "ln1_do": apply_on_vector(1), "ln2_do": apply_on_vector(2), "ln3_do": apply_on_vector(3), "t1_lo": t1_lo,
                     "t2_lo": t2_lo, "pv_lo": pv_lo,
                     "qk_lo": qk_lo, "v": v, "op": op, "feat": feat, "kv": kv, "xs": xs, "xn": xn_, "fc": fc,
                     "mix": mix, "fk": fk, "fv": fv}
            for g, stages in steps:
                n, _, pair = lagged(g)
                if pair is not None:
                    ot_low(pair)
                if 0 <= g < TILES:
                    maxima(g)
                if n is not None:
                    row_sums(n)
                for name, b, args in stages:
                    if name in parts:
                        parts[name](b, *args)

        @block.gpsimd
        def _(pool):
            pool.memset(fm_sb[:, :, :, :, :], 0.0).then_inc(fm_zero, 1)
            pool.memset(power[:, :], -0.5).then_inc(pool_chain, 1)
            pool.memset(kblk[:, :, :, :], 0.0).then_inc(pool_chain, 1)
            pool.memset(xt3[:, :, 0:1], 0.0).then_inc(consts_set, 1)
            pool.wait_ge(pool_chain, 2)

            def scale_values(n):
                m, p = n % NT, (n // NT) % NP
                pool.wait_ge(rsum_ready, n + 1)
                if p % 4 == 0:
                    wait_emptied(pool, ("v", n // (NT * NP), (p // 4, m)))
                pool.tensor_tensor(v_sb[:, m, 2 * p:2 * p + 2, :], v_sb[:, m, 2 * p:2 * p + 2, :],
                                   rsum[:, n % 4, :].unsqueeze(2).broadcast_to([P, 2, VD]), ALU.mult)\
                    .then_inc(v_scaled, 1)

            def norm_apply(k):
                def ln(b, half):
                    i = k > 1
                    count = 2 * b + half if k == 1 else 4 * b + 2 * (k - 2) + half
                    pool.wait_ge(var_ready[i], count + 1)
                    pool.tensor_tensor(rstd[i][:, count % 2, :], veps[i][:, count % 2, :], power[:, :], ALU.pow).then_inc(rstd_ready[i], 1)
                    if not on_vector(k, b):
                        apply_norm(pool, k, b, half)
                    if k == 2:
                        pool.wait_ge(xn_ready[i], count + 1)
                        if count == 0:
                            pool.wait_ge(post_in, 48)
                        at = x_at(b, half)
                        pool.tensor_tensor(x_sb[:, at:at + 2, :], x_sb[:, at:at + 2, :],
                                           fcb[:, :].unsqueeze(1).broadcast_to([P, 2, D]), ALU.add)\
                            .then_inc(bias_added, 1)
                return ln

            def xn_(b, t, gg):
                n = 8 * b + 2 * t + gg
                pool.wait_ge(xrec_ready, n + 1)
                sx3 = x_tile(n).rearrange("p (h l) -> p h l", h=8)
                pool.tensor_tensor(sx3, sx3, xrec[:, n % 4, :].unsqueeze(2).broadcast_to([P, 8, L]), ALU.mult)\
                    .then_inc(xp_ready, 1)

            def fk(b, half):
                if b == B - 1:
                    return
                wait_emptied(pool, ("fk", b, (half,)))
                pool.tensor_tensor(kact[:, :, :], kact[:, :, :], kact[:, :, :], ALU.mult).then_inc(kact_ready, 1)

            parts = {"ln1": norm_apply(1), "ln2": norm_apply(2), "ln3": norm_apply(3), "xn": xn_, "fk": fk}
            for g, stages in steps:
                n, _, _ = lagged(g)
                if n is not None:
                    scale_values(n)
                for name, b, args in stages:
                    if name in parts:
                        parts[name](b, *args)


def kernel(x, ctx_1024, L0_attn_query_proj, L0_attn_key_proj, L0_attn_value_proj, L0_attn_output_proj,
           L0_xattn_fm_w, L0_xattn_fm_b, L0_xattn_fc_w, L0_xattn_fc_b, L0_ffn_W_r, L0_ffn_W_k, L0_ffn_W_v,
           L0_ffn_mu_r, L0_ffn_mu_k):
    import numpy as np
    import concourse.bacc as bacc
    from concourse.bass_utils import run_bass_kernel_spmd

    def rows(a, c):
        return np.ascontiguousarray(np.reshape(a, (c, P, -1)).transpose(1, 0, 2))

    wq = np.asarray(L0_attn_query_proj).transpose(2, 1, 0).reshape(D, H * KD)
    wk = np.asarray(L0_attn_key_proj).transpose(2, 0, 1).reshape(D, H * KD)
    arrays = {
        "x": np.asarray(x).reshape(B * N, D),
        "ctx_t": rows(np.asarray(ctx_1024).transpose(2, 0, 1).reshape(D, B * L), DC),
        "wqk": rows(np.concatenate([wq, wk], axis=1), DC),
        "wv": rows(np.asarray(L0_attn_value_proj).transpose(2, 0, 1).reshape(D, H * VD), DC),
        "wo": rows(np.asarray(L0_attn_output_proj).transpose(1, 2, 0).reshape(H * VD, D), NP),
        "fm_t": np.ascontiguousarray(np.asarray(L0_xattn_fm_w).T),
        "fm_b": np.asarray(L0_xattn_fm_b).reshape(KD, 1),
        "wfc": rows(np.asarray(L0_xattn_fc_w).T, 4),
        "fc_b": np.asarray(L0_xattn_fc_b),
        "wffn": np.ascontiguousarray(np.stack([rows(np.asarray(w).T, DC) for w in (L0_ffn_W_r, L0_ffn_W_k, L0_ffn_W_v)], axis=1)),
        "mu": np.ascontiguousarray(np.stack([np.asarray(m).reshape(DC, P).T for m in (L0_ffn_mu_r, L0_ffn_mu_k)], axis=1)),
        "ident": np.eye(P, dtype=np.float32),
        "sign": np.tile(np.repeat(np.array([1.0, -1.0], np.float32), KD), 4).reshape(P, 1),
    }
    nc = bacc.Bacc("TRN2", target_bir_lowering=False, num_devices=1)
    aps = {k: nc.dram_tensor(f"in_{k}", a.shape, mybir.dt.from_np(a.dtype), kind="ExternalInput").ap()
           for k, a in arrays.items()}
    aps["out"] = nc.dram_tensor("out", (B * N, D), F32, kind="ExternalOutput").ap()
    build(nc, **aps)
    r = run_bass_kernel_spmd(nc, [{f"in_{k}": a for k, a in arrays.items()}], core_ids=[0])
    return r.results[0]["out"].reshape(B, N, D)
```
